# Optimizing a Trainium2 kernel written in Bass

```python
import numpy as np
import jax
import jax.numpy as jnp

def _softmax(x, axis=-1):
    return jax.nn.softmax(x, axis=axis)

def _gelu(x):
    return jax.nn.gelu(x, approximate=True)

def _silu(x):
    return jax.nn.silu(x)

def _sigmoid(x):
    return jax.nn.sigmoid(x)

def _layernorm(x, axis=-1, eps=1e-05):
    m = jnp.mean(x, axis=axis, keepdims=True)
    v = jnp.var(x, axis=axis, keepdims=True)
    return (x - m) / jnp.sqrt(v + eps)

def _scatter_add(tgt, idx, src, axis=0):
    return tgt.at[idx].add(src)

def _segment_sum(src, seg, n):
    return jax.ops.segment_sum(src, seg, n)
kernel_name = 'mk_dlrm_tower_d1_rec_r8_d0b268'

def setup_inputs(seed: int=0):
    np.random.seed(seed)
    _w = jnp.asarray

    def _rec_inputs():
        import jax
        import jax.numpy as jnp
        _tk = jax.random.key(seed)
        dense_ctx = jax.random.normal(jax.random.fold_in(_tk, 190), (512, 16), jnp.float32)
        ids = jnp.stack([jax.random.randint(jax.random.fold_in(_tk, 200 + f), (512,), 0, v, jnp.int32) for f, v in enumerate([125000, 1250, 1000, 125000, 1000, 1250, 1250, 125000, 1000, 125000, 1000, 12500, 1000, 1000, 12500, 12500, 125000, 12500, 12500, 1000, 125000, 1000, 125000, 125000, 1000, 1000, 1000, 12500, 125000, 12500, 1000, 1000, 12500, 1250, 125000, 12500, 125000, 1250, 1250])], axis=1)
        tbl_0 = 0.05 * jax.random.normal(jax.random.fold_in(_tk, 500 + 0), (125000, 16), jnp.float32)
        tbl_1 = 0.05 * jax.random.normal(jax.random.fold_in(_tk, 500 + 1), (1250, 16), jnp.float32)
        tbl_2 = 0.05 * jax.random.normal(jax.random.fold_in(_tk, 500 + 2), (1000, 16), jnp.float32)
        tbl_3 = 0.05 * jax.random.normal(jax.random.fold_in(_tk, 500 + 3), (125000, 16), jnp.float32)
        tbl_4 = 0.05 * jax.random.normal(jax.random.fold_in(_tk, 500 + 4), (1000, 16), jnp.float32)
        tbl_5 = 0.05 * jax.random.normal(jax.random.fold_in(_tk, 500 + 5), (1250, 16), jnp.float32)
        tbl_6 = 0.05 * jax.random.normal(jax.random.fold_in(_tk, 500 + 6), (1250, 16), jnp.float32)
        tbl_7 = 0.05 * jax.random.normal(jax.random.fold_in(_tk, 500 + 7), (125000, 16), jnp.float32)
        tbl_8 = 0.05 * jax.random.normal(jax.random.fold_in(_tk, 500 + 8), (1000, 16), jnp.float32)
        tbl_9 = 0.05 * jax.random.normal(jax.random.fold_in(_tk, 500 + 9), (125000, 16), jnp.float32)
        tbl_10 = 0.05 * jax.random.normal(jax.random.fold_in(_tk, 500 + 10), (1000, 16), jnp.float32)
        tbl_11 = 0.05 * jax.random.normal(jax.random.fold_in(_tk, 500 + 11), (12500, 16), jnp.float32)
        tbl_12 = 0.05 * jax.random.normal(jax.random.fold_in(_tk, 500 + 12), (1000, 16), jnp.float32)
        tbl_13 = 0.05 * jax.random.normal(jax.random.fold_in(_tk, 500 + 13), (1000, 16), jnp.float32)
        tbl_14 = 0.05 * jax.random.normal(jax.random.fold_in(_tk, 500 + 14), (12500, 16), jnp.float32)
        tbl_15 = 0.05 * jax.random.normal(jax.random.fold_in(_tk, 500 + 15), (12500, 16), jnp.float32)
        tbl_16 = 0.05 * jax.random.normal(jax.random.fold_in(_tk, 500 + 16), (125000, 16), jnp.float32)
        tbl_17 = 0.05 * jax.random.normal(jax.random.fold_in(_tk, 500 + 17), (12500, 16), jnp.float32)
        tbl_18 = 0.05 * jax.random.normal(jax.random.fold_in(_tk, 500 + 18), (12500, 16), jnp.float32)
        tbl_19 = 0.05 * jax.random.normal(jax.random.fold_in(_tk, 500 + 19), (1000, 16), jnp.float32)
        tbl_20 = 0.05 * jax.random.normal(jax.random.fold_in(_tk, 500 + 20), (125000, 16), jnp.float32)
        tbl_21 = 0.05 * jax.random.normal(jax.random.fold_in(_tk, 500 + 21), (1000, 16), jnp.float32)
        tbl_22 = 0.05 * jax.random.normal(jax.random.fold_in(_tk, 500 + 22), (125000, 16), jnp.float32)
        tbl_23 = 0.05 * jax.random.normal(jax.random.fold_in(_tk, 500 + 23), (125000, 16), jnp.float32)
        tbl_24 = 0.05 * jax.random.normal(jax.random.fold_in(_tk, 500 + 24), (1000, 16), jnp.float32)
        tbl_25 = 0.05 * jax.random.normal(jax.random.fold_in(_tk, 500 + 25), (1000, 16), jnp.float32)
        tbl_26 = 0.05 * jax.random.normal(jax.random.fold_in(_tk, 500 + 26), (1000, 16), jnp.float32)
        tbl_27 = 0.05 * jax.random.normal(jax.random.fold_in(_tk, 500 + 27), (12500, 16), jnp.float32)
        tbl_28 = 0.05 * jax.random.normal(jax.random.fold_in(_tk, 500 + 28), (125000, 16), jnp.float32)
        tbl_29 = 0.05 * jax.random.normal(jax.random.fold_in(_tk, 500 + 29), (12500, 16), jnp.float32)
        tbl_30 = 0.05 * jax.random.normal(jax.random.fold_in(_tk, 500 + 30), (1000, 16), jnp.float32)
        tbl_31 = 0.05 * jax.random.normal(jax.random.fold_in(_tk, 500 + 31), (1000, 16), jnp.float32)
        tbl_32 = 0.05 * jax.random.normal(jax.random.fold_in(_tk, 500 + 32), (12500, 16), jnp.float32)
        tbl_33 = 0.05 * jax.random.normal(jax.random.fold_in(_tk, 500 + 33), (1250, 16), jnp.float32)
        tbl_34 = 0.05 * jax.random.normal(jax.random.fold_in(_tk, 500 + 34), (125000, 16), jnp.float32)
        tbl_35 = 0.05 * jax.random.normal(jax.random.fold_in(_tk, 500 + 35), (12500, 16), jnp.float32)
        tbl_36 = 0.05 * jax.random.normal(jax.random.fold_in(_tk, 500 + 36), (125000, 16), jnp.float32)
        tbl_37 = 0.05 * jax.random.normal(jax.random.fold_in(_tk, 500 + 37), (1250, 16), jnp.float32)
        tbl_38 = 0.05 * jax.random.normal(jax.random.fold_in(_tk, 500 + 38), (1250, 16), jnp.float32)
        _rk = jax.random.fold_in(_tk, 7)
        W_top1 = 0.0606339 * jax.random.normal(jax.random.fold_in(_tk, 801), (272, 512), jnp.float32)
        W_top2 = 0.0441942 * jax.random.normal(jax.random.fold_in(_tk, 802), (512, 256), jnp.float32)
        W_top3 = 0.0625 * jax.random.normal(jax.random.fold_in(_tk, 803), (256, 1), jnp.float32)
        b_top1 = jnp.zeros((512,), jnp.float32)
        b_top2 = jnp.zeros((256,), jnp.float32)
        return (dense_ctx, ids, tbl_0, tbl_1, tbl_2, tbl_3, tbl_4, tbl_5, tbl_6, tbl_7, tbl_8, tbl_9, tbl_10, tbl_11, tbl_12, tbl_13, tbl_14, tbl_15, tbl_16, tbl_17, tbl_18, tbl_19, tbl_20, tbl_21, tbl_22, tbl_23, tbl_24, tbl_25, tbl_26, tbl_27, tbl_28, tbl_29, tbl_30, tbl_31, tbl_32, tbl_33, tbl_34, tbl_35, tbl_36, tbl_37, tbl_38, W_top1, b_top1, W_top2, b_top2, W_top3)
    dense_ctx, ids, tbl_0, tbl_1, tbl_2, tbl_3, tbl_4, tbl_5, tbl_6, tbl_7, tbl_8, tbl_9, tbl_10, tbl_11, tbl_12, tbl_13, tbl_14, tbl_15, tbl_16, tbl_17, tbl_18, tbl_19, tbl_20, tbl_21, tbl_22, tbl_23, tbl_24, tbl_25, tbl_26, tbl_27, tbl_28, tbl_29, tbl_30, tbl_31, tbl_32, tbl_33, tbl_34, tbl_35, tbl_36, tbl_37, tbl_38, W_top1, b_top1, W_top2, b_top2, W_top3 = _rec_inputs()

    def _L0_rec_setup():
        import jax, jax.numpy as jnp
        import numpy as np
        B, M0, D = (256, 39, 16)
        CIN_SIZE = [128, 128]

        def _cin(inputs, weights):
            X0 = inputs
            Xi = inputs
            res = []
            for W in weights:
                mi = Xi.shape[1]
                z = jnp.einsum('bmd,bnd->bdmn', X0, Xi)
                z = z.reshape(z.shape[0], z.shape[1], M0 * mi)
                Xi = jnp.einsum('bdp,po->bod', z, W)
                res.append(Xi)
            res = jnp.concatenate(res, axis=1)
            return jnp.sum(res, axis=-1)
        key = jax.random.key(seed)
        k1, k2, k3 = jax.random.split(key, 3)
        inputs = jax.random.normal(k1, (B, M0, D), dtype=jnp.float32)
        W0 = jax.random.normal(k2, (M0 * M0, CIN_SIZE[0]), dtype=jnp.float32) * 0.05
        W1 = jax.random.normal(k3, (M0 * CIN_SIZE[0], CIN_SIZE[1]), dtype=jnp.float32) * 0.05
        return {'inputs': inputs, 'W0': W0, 'W1': W1}
    _L0_rec_all = _L0_rec_setup()
    _L0_rec_in = {k: v for k, v in _L0_rec_all.items() if k in ('W0', 'W1')}
    del _L0_rec_all
    return {'dense_ctx': dense_ctx, 'ids': ids, 'tbl_0': tbl_0, 'tbl_1': tbl_1, 'tbl_2': tbl_2, 'tbl_3': tbl_3, 'tbl_4': tbl_4, 'tbl_5': tbl_5, 'tbl_6': tbl_6, 'tbl_7': tbl_7, 'tbl_8': tbl_8, 'tbl_9': tbl_9, 'tbl_10': tbl_10, 'tbl_11': tbl_11, 'tbl_12': tbl_12, 'tbl_13': tbl_13, 'tbl_14': tbl_14, 'tbl_15': tbl_15, 'tbl_16': tbl_16, 'tbl_17': tbl_17, 'tbl_18': tbl_18, 'tbl_19': tbl_19, 'tbl_20': tbl_20, 'tbl_21': tbl_21, 'tbl_22': tbl_22, 'tbl_23': tbl_23, 'tbl_24': tbl_24, 'tbl_25': tbl_25, 'tbl_26': tbl_26, 'tbl_27': tbl_27, 'tbl_28': tbl_28, 'tbl_29': tbl_29, 'tbl_30': tbl_30, 'tbl_31': tbl_31, 'tbl_32': tbl_32, 'tbl_33': tbl_33, 'tbl_34': tbl_34, 'tbl_35': tbl_35, 'tbl_36': tbl_36, 'tbl_37': tbl_37, 'tbl_38': tbl_38, 'W_top1': W_top1, 'b_top1': b_top1, 'W_top2': W_top2, 'b_top2': b_top2, 'W_top3': W_top3, 'L0_rec_W0': _L0_rec_in['W0'], 'L0_rec_W1': _L0_rec_in['W1']}

def reference(dense_ctx, ids, tbl_0, tbl_1, tbl_2, tbl_3, tbl_4, tbl_5, tbl_6, tbl_7, tbl_8, tbl_9, tbl_10, tbl_11, tbl_12, tbl_13, tbl_14, tbl_15, tbl_16, tbl_17, tbl_18, tbl_19, tbl_20, tbl_21, tbl_22, tbl_23, tbl_24, tbl_25, tbl_26, tbl_27, tbl_28, tbl_29, tbl_30, tbl_31, tbl_32, tbl_33, tbl_34, tbl_35, tbl_36, tbl_37, tbl_38, W_top1, b_top1, W_top2, b_top2, W_top3, L0_rec_W0, L0_rec_W1):
    import jax
    import jax.numpy as jnp

    def _L0_rec_ref(inputs, W0, W1):
        import jax, jax.numpy as jnp
        import numpy as np
        B, M0, D = (256, 39, 16)
        CIN_SIZE = [128, 128]

        def _cin(inputs, weights):
            X0 = inputs
            Xi = inputs
            res = []
            for W in weights:
                mi = Xi.shape[1]
                z = jnp.einsum('bmd,bnd->bdmn', X0, Xi)
                z = z.reshape(z.shape[0], z.shape[1], M0 * mi)
                Xi = jnp.einsum('bdp,po->bod', z, W)
                res.append(Xi)
            res = jnp.concatenate(res, axis=1)
            return jnp.sum(res, axis=-1)
        return _cin(inputs, [W0, W1])
    e = jnp.stack([tbl_0[ids[:, 0]], tbl_1[ids[:, 1]], tbl_2[ids[:, 2]], tbl_3[ids[:, 3]], tbl_4[ids[:, 4]], tbl_5[ids[:, 5]], tbl_6[ids[:, 6]], tbl_7[ids[:, 7]], tbl_8[ids[:, 8]], tbl_9[ids[:, 9]], tbl_10[ids[:, 10]], tbl_11[ids[:, 11]], tbl_12[ids[:, 12]], tbl_13[ids[:, 13]], tbl_14[ids[:, 14]], tbl_15[ids[:, 15]], tbl_16[ids[:, 16]], tbl_17[ids[:, 17]], tbl_18[ids[:, 18]], tbl_19[ids[:, 19]], tbl_20[ids[:, 20]], tbl_21[ids[:, 21]], tbl_22[ids[:, 22]], tbl_23[ids[:, 23]], tbl_24[ids[:, 24]], tbl_25[ids[:, 25]], tbl_26[ids[:, 26]], tbl_27[ids[:, 27]], tbl_28[ids[:, 28]], tbl_29[ids[:, 29]], tbl_30[ids[:, 30]], tbl_31[ids[:, 31]], tbl_32[ids[:, 32]], tbl_33[ids[:, 33]], tbl_34[ids[:, 34]], tbl_35[ids[:, 35]], tbl_36[ids[:, 36]], tbl_37[ids[:, 37]], tbl_38[ids[:, 38]]], axis=1)
    z = _L0_rec_ref(e, L0_rec_W0, L0_rec_W1)
    z = z.reshape(z.shape[0], -1)
    h = jnp.concatenate([z, dense_ctx], axis=1)
    h = jnp.maximum(h @ W_top1 + b_top1, 0.0)
    h = jnp.maximum(h @ W_top2 + b_top2, 0.0)
    y = h @ W_top3
    return y

_drawn_inputs = setup_inputs


def setup_inputs(seed=0):
    import zlib

    import numpy as np

    out = dict(_drawn_inputs(seed))
    spreads = {'b_top1': (0.0, 0.1), 'b_top2': (0.0, 0.1)}
    factors = {'tbl_0': 4.528,
     'tbl_1': 5.113,
     'tbl_2': 4.88,
     'tbl_3': 4.982,
     'tbl_4': 5.242,
     'tbl_5': 5.558,
     'tbl_6': 4.985,
     'tbl_7': 4.975,
     'tbl_8': 5.072,
     'tbl_9': 5.001,
     'tbl_10': 5.201,
     'tbl_11': 4.855,
     'tbl_12': 4.765,
     'tbl_13': 4.942,
     'tbl_14': 4.646,
     'tbl_15': 5.207,
     'tbl_16': 5.076,
     'tbl_17': 4.831,
     'tbl_18': 5.18,
     'tbl_19': 5.229,
     'tbl_20': 5.091,
     'tbl_21': 5.057,
     'tbl_22': 5.211,
     'tbl_23': 5.025,
     'tbl_24': 5.031,
     'tbl_25': 4.395,
     'tbl_26': 5.092,
     'tbl_27': 4.969,
     'tbl_28': 4.978,
     'tbl_29': 4.966,
     'tbl_30': 4.863,
     'tbl_31': 4.729,
     'tbl_32': 5.135,
     'tbl_33': 4.865,
     'tbl_34': 4.935,
     'tbl_35': 5.003,
     'tbl_36': 4.978,
     'tbl_37': 5.017,
     'tbl_38': 5.188,
     'L0_rec_W1': 5.544}
    for name, (base, spread) in spreads.items():
        noise = np.random.default_rng([zlib.crc32(name.encode()), seed]).standard_normal(out[name].shape)
        drawn = base * np.exp(spread * noise) if base else spread * noise
        out[name] = jnp.asarray(drawn.astype(out[name].dtype))
    for name, factor in factors.items():
        out[name] = (out[name] * factor).astype(out[name].dtype)
    return out
```

```python
from contextlib import ExitStack

import concourse.bass as bass
from concourse import mybir

F32 = mybir.dt.float32
BF16 = mybir.dt.bfloat16
I32 = mybir.dt.int32
ALU = mybir.AluOpType
ACT = mybir.ActivationFunctionType

BATCH, FIELDS, DIM, MAPS = 512, 39, 16, 128
DENSE, HID1, HID2 = 16, 512, 256
TILE = 128
TURNS, HALVES = 2, 2
TURN_ROWS = HALVES * TILE
SHIFTS = FIELDS // 2 + 1
PER_PASS = 3
ROWS = PER_PASS * FIELDS
PASSES = -(-SHIFTS // PER_PASS)
LAST_ROWS = (SHIFTS - PER_PASS * (PASSES - 1)) * FIELDS
UNITS = 4
UNIT = TILE // UNITS * DIM
UNIT_D = DIM // UNITS
CHUNK = 128 // DIM
CHUNKS = TILE // CHUNK
AUG = FIELDS + 1
PRODUCTS = 3


def build(nc, ids, tables, W0_pairs, W0_mirror, W1, dense_t, W_top1, b_top1, W_top2, b_top2, W_top3,
          rotations, eye, same_row, out):
    ctx = ExitStack()
    with ctx:
        def sb(name, shape, dt=F32):
            return ctx.enter_context(nc.sbuf_tensor(name, shape, dt))

        def ring(name, n=2):
            return [ctx.enter_context(nc.psum_tensor(f"{name}{i}", [128, 512], F32)) for i in range(n)]

        def sem(name):
            return ctx.enter_context(nc.semaphore(name))

        ids_sb = sb("ids_sb", [TILE, TURNS * HALVES, FIELDS], I32)
        rot_f32 = sb("rot_f32", [ROWS, (1 + PASSES) * ROWS])
        rot = sb("rot", [ROWS, 1 + PASSES, ROWS], BF16)
        eye_sb = sb("eye_sb", [128, 128])
        eye_bf = sb("eye_bf", [128, 128], BF16)
        same_sb = sb("same_sb", [128, CHUNK])
        pair_w = sb("pair_w", [ROWS, PASSES, MAPS])
        mirror_w = sb("mirror_w", [ROWS, PASSES, MAPS])
        w1_sb = sb("w1_sb", [MAPS, FIELDS, MAPS])
        wt1 = sb("wt1", [128, 2, HID1])
        wt1_dense = sb("wt1_dense", [DENSE, HID1])
        wt2 = sb("wt2", [128, HID1 // 128, HID2])
        wt3 = sb("wt3", [128, HID2 // 128])
        bt1 = sb("bt1", [128, HID1 // 128])
        bt2 = sb("bt2", [128, HID2 // 128])
        dense_sb = sb("dense_sb", [DENSE, BATCH])

        emb = [sb(f"emb{p}", [TILE, FIELDS, DIM]) for p in range(HALVES)]
        rest = sb("rest", [TILE, FIELDS, DIM])
        parts = sb("parts", [TILE, DIM, ROWS], BF16)
        parts_t = sb("parts_t", [ROWS, TILE, DIM], BF16)
        left = sb("left", [ROWS, TILE * DIM])
        prod = [sb(f"prod{i}", [ROWS, UNIT]) for i in range(PRODUCTS)]
        x1 = sb("x1", [MAPS, TILE * DIM])
        x1_t = [sb(f"x1_t{i}", [128, MAPS]) for i in range(2)]
        blocks = [sb(f"blocks{i}", [128, CHUNK, AUG]) for i in range(2)]
        gram = sb("gram", [MAPS, AUG, TURN_ROWS])
        z2 = sb("z2", [MAPS, TURN_ROWS])
        h1 = sb("h1", [128, HID1 // 128, TURN_ROWS])
        h2 = sb("h2", [128, HID2 // 128, TURN_ROWS])
        y_sb = sb("y_sb", [1, BATCH])

        ring_b = ring("ring_b")
        ring_t = ring("ring_t")
        ring_x = ring("ring_x")
        ring_g = ring("ring_g")
        B_TILE, T_TILE, X_TILE, G_TILE = UNITS * PASSES + CHUNKS, 2 * UNITS + CHUNKS, UNITS, CHUNKS
        B_TURN, T_TURN = HALVES * B_TILE, HALVES * T_TILE
        X_TURN = HALVES * X_TILE + HID1 // 128 + HID2 // 128
        G_TURN = HALVES * G_TILE + 2

        ids_in = sem("ids_in")
        consts_in = sem("consts_in")
        pairs_in = sem("pairs_in")
        w1_in = sem("w1_in")
        top_in = sem("top_in")
        out_done = sem("out_done")
        gathered = [sem(f"gathered{p}") for p in range(HALVES)]
        emb_free = sem("emb_free")
        split_step = sem("split_step")
        parts_ready = sem("parts_ready")
        consts_ready = sem("consts_ready")
        pair_w_ready = sem("pair_w_ready")
        b_full, b_done = sem("b_full"), sem("b_done")
        t_full, t_done = sem("t_full"), sem("t_done")
        x_full, x_done = sem("x_full"), sem("x_done")
        g_full, g_done = sem("g_full"), sem("g_done")
        FREE = 2

        block = ctx.enter_context(nc.Block())

        def b_product(h, p, u, k):
            return h * B_TURN + (p * B_TILE + u * PASSES + k)

        def b_field(h, p, c):
            return h * B_TURN + (p * B_TILE + UNITS * PASSES + c)

        def t_parts(h, p, u):
            return h * T_TURN + (p * T_TILE + u)

        def t_left(h, p, u):
            return h * T_TURN + (p * T_TILE + UNITS + u)

        def t_x1(h, p, c):
            return h * T_TURN + (p * T_TILE + 2 * UNITS + c)

        def x_unit(h, p, u):
            return h * X_TURN + (p * X_TILE + u)

        def x_hid(h, k):
            return h * X_TURN + (HALVES * X_TILE + k)

        def g_chunk(h, p, c):
            return h * G_TURN + (p * G_TILE + c)

        def g_tail(h, k):
            return h * G_TURN + (HALVES * G_TILE + k)

        def bank(banks, fill_in_turn):
            return banks[fill_in_turn % 2]

        @block.sync
        def _(sp):
            sp.dma_start(ids_sb[:, :, :], ids.rearrange("(t p) f -> p t f", p=TILE)).then_inc(ids_in, 16)
            sp.dma_start(rot_f32[:, :], rotations).then_inc(consts_in, 16)
            sp.dma_start(eye_sb[:, :], eye).then_inc(consts_in, 16)
            sp.dma_start(same_sb[:, :], same_row).then_inc(consts_in, 16)
            full = (PASSES - 1) * ROWS
            for dst, src in ((pair_w, W0_pairs), (mirror_w, W0_mirror)):
                sp.dma_start(dst[:, 0:PASSES - 1, :],
                             src[0:full, :].rearrange("(t p) o -> p t o", p=ROWS)).then_inc(pairs_in, 16)
                sp.dma_start(dst[0:LAST_ROWS, PASSES - 1, :], src[full:full + LAST_ROWS, :]).then_inc(pairs_in, 16)
            sp.dma_start(w1_sb[:, :, :], W1.rearrange("(m n) o -> n m o", n=MAPS)).then_inc(w1_in, 16)
            sp.dma_start(wt1[:, :, :], W_top1[0:2 * MAPS, :].rearrange("(k p) h -> p k h", p=128)).then_inc(top_in, 16)
            sp.dma_start(wt1_dense[:, :], W_top1[2 * MAPS:2 * MAPS + DENSE, :]).then_inc(top_in, 16)
            sp.dma_start(wt2[:, :, :], W_top2.rearrange("(k p) h -> p k h", p=128)).then_inc(top_in, 16)
            sp.dma_start(wt3[:, :], W_top3).then_inc(top_in, 16)
            sp.dma_start(bt1[:, :], b_top1).then_inc(top_in, 16)
            sp.dma_start(bt2[:, :], b_top2).then_inc(top_in, 16)
            sp.dma_start(dense_sb[:, :], dense_t).then_inc(top_in, 16)
            sp.wait_ge(g_done, TURNS * G_TURN + FREE)
            sp.dma_start(out.rearrange("b one -> one b"), y_sb[:, :]).then_inc(out_done, 16)
            sp.wait_ge(out_done, 16)

        @block.gpsimd
        def _(pool):
            pool.wait_ge(ids_in, 16)
            for t in range(TURNS * HALVES):
                if t >= HALVES:
                    pool.wait_ge(emb_free, t - HALVES + 1)
                for f in range(FIELDS):
                    nc.gpsimd.indirect_dma_start(
                        emb[t % HALVES][:, f, :], None, tables[f],
                        bass.IndirectOffsetOnAxis(ap=ids_sb[:, t, f:f + 1], axis=0)).then_inc(gathered[t % HALVES], 16)

        @block.vector
        def _(dve):
            steps = 0

            def step(ins):
                nonlocal steps
                steps += 1
                ins.then_inc(split_step, 1)
                dve.wait_ge(split_step, steps)

            dve.sem_inc(b_done, FREE)
            dve.wait_ge(consts_in, 48)
            nc.vector.tensor_copy(rot[:, :, :], rot_f32[:, :].rearrange("p (k q) -> p k q", q=ROWS)).then_inc(consts_ready, 1)
            nc.vector.tensor_copy(eye_bf[:, :], eye_sb[:, :]).then_inc(consts_ready, 1)
            for buf in blocks:
                nc.vector.tensor_copy(buf[:, :, FIELDS:AUG].rearrange("p c one -> p (c one)"), same_sb[:, :]).then_inc(consts_ready, 1)
            dve.wait_ge(pairs_in, 64)
            nc.vector.tensor_tensor(pair_w[:, 1:PASSES - 1, :], pair_w[:, 1:PASSES - 1, :],
                                    mirror_w[:, 1:PASSES - 1, :], ALU.add).then_inc(pair_w_ready, 1)
            nc.vector.tensor_tensor(pair_w[0:LAST_ROWS, PASSES - 1, :], pair_w[0:LAST_ROWS, PASSES - 1, :],
                                    mirror_w[0:LAST_ROWS, PASSES - 1, :], ALU.add).then_inc(pair_w_ready, 1)
            step(nc.vector.tensor_tensor(pair_w[:, 0, :], pair_w[:, 0, :], mirror_w[:, 0, :], ALU.add))
            nc.vector.tensor_scalar(pair_w[0:FIELDS, 0, :], pair_w[0:FIELDS, 0, :], 0.5, None, ALU.mult).then_inc(pair_w_ready, 1)

            SPLIT = 3
            with dve.Fori(0, TURNS) as h:
                for p in range(HALVES):
                    dve.wait_ge(gathered[p], (h + 1) * (16 * FIELDS))
                    first = steps + p * SPLIT
                    high, mid, low = (parts[:, :, i * FIELDS:(i + 1) * FIELDS].rearrange("b d m -> b m d")
                                      for i in range(3))
                    nc.vector.tensor_copy(high, emb[p][:, :, :]).then_inc(split_step, 1)
                    dve.wait_ge(split_step, h * (SPLIT * HALVES) + (first + 1))
                    nc.vector.tensor_tensor(rest[:, :, :], emb[p][:, :, :], high, ALU.subtract).then_inc(split_step, 1)
                    dve.wait_ge(split_step, h * (SPLIT * HALVES) + (first + 2))
                    nc.vector.tensor_copy(mid, rest[:, :, :]).then_inc(split_step, 1)
                    dve.wait_ge(split_step, h * (SPLIT * HALVES) + (first + 3))
                    dve.sem_inc(emb_free, 1)
                    nc.vector.tensor_tensor(low, rest[:, :, :], mid, ALU.subtract).then_inc(parts_ready, 1)
                    for u in range(UNITS):
                        dve.wait_ge(t_done, t_left(h, p, u) + (FREE + 1))
                        lhs = left[:, u * UNIT:(u + 1) * UNIT]
                        for k in range(PASSES):
                            n = b_product(0, p, u, k)
                            rows = ROWS if k < PASSES - 1 else LAST_ROWS
                            dve.wait_ge(b_full, b_product(h, p, u, k) + 1)
                            nc.vector.tensor_tensor(prod[(u * PASSES + k) % PRODUCTS][0:rows, :], lhs[0:rows, :],
                                                    bank(ring_b, n)[0:rows, :], ALU.mult).then_inc(b_done, 1)
                    for c in range(CHUNKS):
                        dve.wait_ge(b_full, b_field(h, p, c) + 1)
                        fields = bank(ring_b, b_field(0, p, c))[:, 0:FIELDS]
                        nc.vector.tensor_tensor(blocks[c % 2][:, :, 0:FIELDS],
                                                fields.unsqueeze(1).to_broadcast([128, CHUNK, FIELDS]),
                                                same_sb[:, :].unsqueeze(2).to_broadcast([128, CHUNK, FIELDS]),
                                                ALU.mult).then_inc(b_done, 1)

        @block.scalar
        def _(act):
            act.sem_inc(t_done, FREE)
            act.sem_inc(x_done, FREE)
            act.sem_inc(g_done, FREE)
            with act.Fori(0, TURNS) as h:
                for p in range(HALVES):
                    for u in range(UNITS):
                        act.wait_ge(t_full, t_parts(h, p, u) + 1)
                        nc.scalar.copy(parts_t[:, :, u * UNIT_D:(u + 1) * UNIT_D].rearrange("q b d -> q d b"),
                                       bank(ring_t, t_parts(0, p, u))[0:ROWS, 0:UNIT_D * TILE // 2].bitcast(BF16).rearrange(
                                           "q (d b) -> q d b", b=TILE)).then_inc(t_done, 1)

                    def keep_x1(u):
                        act.wait_ge(x_full, x_unit(h, p, u) + 1)
                        nc.scalar.copy(x1[:, u * UNIT:(u + 1) * UNIT],
                                       bank(ring_x, x_unit(0, p, u))[:, :]).then_inc(x_done, 1)

                    def keep_gram(c):
                        act.wait_ge(g_full, g_chunk(h, p, c) + 1)
                        at = p * TILE + c * CHUNK
                        nc.scalar.copy(gram[:, :, at:at + CHUNK],
                                       bank(ring_g, g_chunk(0, p, c))[:, 0:CHUNK * AUG].rearrange(
                                           "n (b m) -> n m b", m=AUG)).then_inc(g_done, 1)

                    for u in range(UNITS):
                        act.wait_ge(t_full, t_left(h, p, u) + 1)
                        nc.scalar.copy(left[:, u * UNIT:(u + 1) * UNIT],
                                       bank(ring_t, t_left(0, p, u))[0:ROWS, :]).then_inc(t_done, 1)
                        if u:
                            keep_x1(u - 1)
                    keep_x1(UNITS - 1)
                    for c in range(CHUNKS):
                        act.wait_ge(t_full, t_x1(h, p, c) + 1)
                        nc.scalar.copy(x1_t[c % 2][:, :], bank(ring_t, t_x1(0, p, c))[:, 0:MAPS]).then_inc(t_done, 1)
                        if c:
                            keep_gram(c - 1)
                    keep_gram(CHUNKS - 1)
                act.wait_ge(g_full, g_tail(h, 0) + 1)
                nc.scalar.copy(z2[:, :], bank(ring_g, g_tail(0, 0))[:, 0:TURN_ROWS]).then_inc(g_done, 1)
                act.wait_ge(top_in, 7 * 16)
                for k in range(HID1 // 128):
                    act.wait_ge(x_full, x_hid(h, k) + 1)
                    nc.scalar.activation(h1[:, k, :], bank(ring_x, x_hid(0, k))[:, 0:TURN_ROWS], ACT.Relu,
                                         bias=bt1[:, k:k + 1]).then_inc(x_done, 1)
                for k in range(HID2 // 128):
                    n = HID1 // 128 + k
                    act.wait_ge(x_full, x_hid(h, n) + 1)
                    nc.scalar.activation(h2[:, k, :], bank(ring_x, x_hid(0, n))[:, 0:TURN_ROWS], ACT.Relu,
                                         bias=bt2[:, k:k + 1]).then_inc(x_done, 1)
                act.wait_ge(g_full, g_tail(h, 1) + 1)
                nc.scalar.copy(y_sb[:, bass.ds(h * TURN_ROWS, TURN_ROWS)],
                               bank(ring_g, g_tail(0, 1))[0:1, 0:TURN_ROWS]).then_inc(g_done, 1)

        @block.tensor
        def _(pe):
            mm = nc.tensor.matmul
            pe.wait_ge(consts_ready, 4)
            with pe.Fori(0, TURNS) as h:
                for p in range(HALVES):
                    pe.wait_ge(parts_ready, h * HALVES + (p + 1))
                    for u in range(UNITS):
                        pe.wait_ge(t_done, t_parts(h, p, u) + 1)
                        dst = bank(ring_t, t_parts(0, p, u))[0:ROWS, 0:UNIT_D * TILE // 2].bitcast(BF16)
                        for i in range(UNIT_D):
                            last = nc.tensor.transpose(dst[:, i * TILE:(i + 1) * TILE], parts[:, u * UNIT_D + i, :], eye_bf[:, :])
                        last.then_inc(t_full, 1)

                    def rotate(u, k):
                        moving = parts_t[:, u * TILE // UNITS:(u + 1) * TILE // UNITS, :].rearrange("q b d -> q (b d)")
                        if k == 0:
                            if u == 0:
                                pe.wait_ge(t_done, t_parts(h, p, UNITS - 1) + (FREE + 1))
                            pe.wait_ge(t_done, t_left(h, p, u) + 1)
                            mm(bank(ring_t, t_left(0, p, u))[0:ROWS, :], rot[:, 0, :], moving,
                               start=True, stop=True).then_inc(t_full, 1)
                        pe.wait_ge(b_done, b_product(h, p, u, k) + 1)
                        mm(bank(ring_b, b_product(0, p, u, k))[0:ROWS, :], rot[:, 1 + k, :], moving,
                           start=True, stop=True).then_inc(b_full, 1)

                    def contract(u, k):
                        rows = ROWS if k < PASSES - 1 else LAST_ROWS
                        if k == 0:
                            pe.wait_ge(x_done, x_unit(h, p, u) + 1)
                        pe.wait_ge(b_done, b_product(h, p, u, k) + (FREE + 1))
                        last = mm(bank(ring_x, x_unit(0, p, u))[:, :], pair_w[0:rows, k, :],
                                  prod[(u * PASSES + k) % PRODUCTS][0:rows, :], start=(k == 0), stop=(k == PASSES - 1))
                        if k == PASSES - 1:
                            last.then_inc(x_full, 1)

                    todo = [(u, k) for u in range(UNITS) for k in range(PASSES)]
                    if p == 0:
                        pe.wait_ge(pair_w_ready, 3)
                    for i, item in enumerate(todo):
                        rotate(*item)
                        if i >= 2:
                            contract(*todo[i - 2])
                    contract(*todo[-2])
                    contract(*todo[-1])

                    def turn_over(c):
                        if c == 0:
                            pe.wait_ge(x_done, x_unit(h, p, UNITS - 1) + (FREE + 1))
                        rows = slice(c * CHUNK * DIM, (c + 1) * CHUNK * DIM)
                        pe.wait_ge(b_done, b_field(h, p, c) + 1)
                        nc.tensor.transpose(bank(ring_b, b_field(0, p, c))[:, 0:ROWS], left[:, rows],
                                            eye_sb[0:ROWS, 0:ROWS]).then_inc(b_full, 1)
                        pe.wait_ge(t_done, t_x1(h, p, c) + 1)
                        nc.tensor.transpose(bank(ring_t, t_x1(0, p, c))[:, 0:MAPS], x1[:, rows],
                                            eye_sb[:, :]).then_inc(t_full, 1)

                    def multiply(c):
                        pe.wait_ge(g_done, g_chunk(h, p, c) + 1)
                        pe.wait_ge(b_done, b_field(h, p, c) + (FREE + 1))
                        pe.wait_ge(t_done, t_x1(h, p, c) + (FREE + 1))
                        mm(bank(ring_g, g_chunk(0, p, c))[:, 0:CHUNK * AUG], x1_t[c % 2][:, :],
                           blocks[c % 2][:, :, :].rearrange("p b m -> p (b m)"), start=True, stop=True).then_inc(g_full, 1)

                    for c in range(CHUNKS):
                        turn_over(c)
                        if c:
                            multiply(c - 1)
                    multiply(CHUNKS - 1)

                pe.wait_ge(w1_in, 16)
                pe.wait_ge(g_done, g_chunk(h, HALVES - 1, CHUNKS - 1) + (FREE + 1))
                acc = bank(ring_g, g_tail(0, 0))[:, 0:TURN_ROWS]
                for m in range(FIELDS):
                    last = mm(acc, w1_sb[:, m, :], gram[:, m, :], start=(m == 0), stop=(m == FIELDS - 1))
                last.then_inc(g_full, 1)

                pe.wait_ge(top_in, 7 * 16)
                pe.wait_ge(g_done, g_tail(h, 0) + (FREE + 1))
                for k in range(HID1 // 128):
                    cols = slice(k * 128, (k + 1) * 128)
                    pe.wait_ge(x_done, x_hid(h, k) + 1)
                    acc = bank(ring_x, x_hid(0, k))[:, 0:TURN_ROWS]
                    mm(acc, wt1[:, 0, cols], gram[:, FIELDS, :], start=True, stop=False)
                    mm(acc, wt1[:, 1, cols], z2[:, :], start=False, stop=False)
                    mm(acc, wt1_dense[:, cols], dense_sb[:, bass.ds(h * TURN_ROWS, TURN_ROWS)], start=False,
                       stop=True).then_inc(x_full, 1)
                pe.wait_ge(x_done, x_hid(h, HID1 // 128 - 1) + (FREE + 1))
                for k in range(HID2 // 128):
                    n = HID1 // 128 + k
                    pe.wait_ge(x_done, x_hid(h, n) + 1)
                    acc = bank(ring_x, x_hid(0, n))[:, 0:TURN_ROWS]
                    for j in range(HID1 // 128):
                        last = mm(acc, wt2[:, j, k * 128:(k + 1) * 128], h1[:, j, :], start=(j == 0), stop=(j == HID1 // 128 - 1))
                    last.then_inc(x_full, 1)
                pe.wait_ge(x_done, x_hid(h, HID1 // 128 + HID2 // 128 - 1) + (FREE + 1))
                pe.wait_ge(g_done, g_tail(h, 1) + 1)
                for j in range(HID2 // 128):
                    last = mm(bank(ring_g, g_tail(0, 1))[0:1, 0:TURN_ROWS], wt3[:, j:j + 1], h2[:, j, :],
                              start=(j == 0), stop=(j == HID2 // 128 - 1))
                last.then_inc(g_full, 1)


def kernel(**inputs):
    import numpy as np
    import concourse.bacc as bacc
    from concourse.bass_utils import run_bass_kernel_spmd

    field = np.arange(ROWS) % FIELDS
    distance = np.arange(ROWS) // FIELDS
    shifts = [0 * distance] + [PER_PASS * k + distance for k in range(PASSES)]
    rotations = np.concatenate([(field[:, None] == (field + s)[None, :] % FIELDS) for s in shifts], axis=1)
    eye = np.eye(128, dtype=np.float32)
    same_row = (np.arange(128)[:, None] // DIM == np.arange(CHUNK)[None, :])

    W0 = np.asarray(inputs["L0_rec_W0"]).reshape(FIELDS, FIELDS, MAPS)
    m = np.tile(np.arange(FIELDS), SHIFTS)
    n = (m + np.repeat(np.arange(SHIFTS), FIELDS)) % FIELDS

    arrays = {
        "ids": np.asarray(inputs["ids"]),
        **{f"tbl_{f}": np.asarray(inputs[f"tbl_{f}"]) for f in range(FIELDS)},
        "W0_pairs": np.ascontiguousarray(W0[m, n]),
        "W0_mirror": np.ascontiguousarray(W0[n, m]),
        "W1": np.asarray(inputs["L0_rec_W1"]),
        "dense_t": np.ascontiguousarray(np.asarray(inputs["dense_ctx"]).T),
        "W_top1": np.asarray(inputs["W_top1"]),
        "W_top2": np.asarray(inputs["W_top2"]),
        **{name: np.ascontiguousarray(np.asarray(inputs[name]).reshape(-1, 128).T)
           for name in ("b_top1", "b_top2", "W_top3")},
        "rotations": rotations.astype(np.float32),
        "eye": eye,
        "same_row": same_row.astype(np.float32),
    }
    nc = bacc.Bacc("TRN2", target_bir_lowering=False, num_devices=1)
    ap = {name: nc.dram_tensor(name, a.shape, mybir.dt.from_np(a.dtype), kind="ExternalInput").ap()
          for name, a in arrays.items()}
    out = nc.dram_tensor("out", (BATCH, 1), F32, kind="ExternalOutput").ap()
    build(nc, ap["ids"], [ap[f"tbl_{f}"] for f in range(FIELDS)], ap["W0_pairs"], ap["W0_mirror"], ap["W1"],
          ap["dense_t"], ap["W_top1"], ap["b_top1"], ap["W_top2"], ap["b_top2"], ap["W_top3"],
          ap["rotations"], ap["eye"], ap["same_row"], out)
    result = run_bass_kernel_spmd(nc, [arrays], core_ids=[0])
    return result.results[0]["out"]
```

```python
from contextlib import ExitStack

import concourse.bass as bass
from concourse import mybir

F32 = mybir.dt.float32
F32R = mybir.dt.float32r
BF16 = mybir.dt.bfloat16
I32 = mybir.dt.int32
ALU = mybir.AluOpType
ACT = mybir.ActivationFunctionType

BATCH, FIELDS, DIM, MAPS = 512, 39, 16, 128
DENSE, HID1, HID2 = 16, 512, 256
H1, H2 = HID1 // 128, HID2 // 128
TILE = 128
TILES = BATCH // TILE
SHIFTS = FIELDS // 2 + 1
PER_PASS = 3
ROWS = PER_PASS * FIELDS
PASSES = -(-SHIFTS // PER_PASS)
LAST_ROWS = (SHIFTS - PER_PASS * (PASSES - 1)) * FIELDS
UNITS = 4
UNIT_B = TILE // UNITS
UNIT = UNIT_B * DIM
PART_D = DIM // UNITS
CHUNK = 128 // DIM
UNIT_CHUNKS = UNIT_B // CHUNK
AUG = FIELDS + 1
SMALL_BLOCKS = 10
SMALL_COLS = SMALL_BLOCKS * DIM
PER_BANK = 512 // SMALL_COLS

ALL = tuple(range(PASSES))
SPLIT = ((), ALL, ALL, ALL)
ROUND_LAG, REMAINDER_LAG, LAG = 1, 2, 4
BUFFERS = LAG + 1
PREPARE_AT = (24, 20, 20)
SUM_GROUP = 3
FINISH_AT = (14, 14, 18)
TURNED = 3


def prepare_steps(t):
    return [[("split", t, i, 0)] for i in range(4)] + [[]] + [[("parts", t, g, 0) for g in range(UNITS)]]


def chunk_steps(t, u):
    own = range(u * UNIT_CHUNKS, (u + 1) * UNIT_CHUNKS)
    stages = ("turn", "spread", "gram")
    return [[]] + [[(kind, t, c - n, 0) for n, kind in enumerate(stages) if c - n in own]
                   for c in range(own[0], own[-1] + len(stages))]


def finish_steps(t):
    return ([[("sum", t, m, 0)] for m in range(0, FIELDS, SUM_GROUP)]
            + [[("hidden", t, k, 0)] for k in range(H1 + H2)] + [[("y", t, 0, 0)]])


def schedule():
    steps = sum(prepare_steps(0), [])
    passes = [(t, u, k) for t in range(TILES) for u in range(UNITS) for k in range(PASSES)]
    prepare, chunks, finish = [], [], []
    at = 0
    while at < len(passes) + LAG or chunks or finish:
        t, i = divmod(at, UNITS * PASSES)
        if t + 1 < TILES and i == PREPARE_AT[t]:
            prepare = prepare_steps(t + 1)
        if 0 < t < TILES and i == FINISH_AT[t - 1]:
            finish = finish_steps(t - 1)
        if t < TILES and i == 0:
            steps += sum(prepare, [])
            prepare = []
        if at < len(passes):
            steps.append(("rotate", *passes[at]))
        for work in (prepare, finish, chunks):
            if work:
                steps += work.pop(0)
        for kind, lag in (("round", ROUND_LAG), ("remainder", REMAINDER_LAG)):
            if lag <= at < len(passes) + lag:
                t, u, k = passes[at - lag]
                if k in SPLIT[t]:
                    steps.append((kind, t, u, k))
        if LAG <= at < len(passes) + LAG:
            t, u, k = passes[at - LAG]
            steps.append(("contract", t, u, k))
            if k == PASSES - 1:
                chunks += chunk_steps(t, u)
        at += 1
    return steps + sum(finish_steps(TILES - 1), [])


STEPS = schedule()


class Fills:

    def __init__(self, banks):
        self.banks, self.number, self.of, self.before, self.last = banks, {}, {}, {}, {}

    def add(self, step, bank):
        self.before[step] = self.last.get(bank)
        self.last[bank] = self.number[step] = len(self.number)
        self.of[step] = self.banks[bank]

    def up_to(self, step):
        return self.number[step] + 1


def build(nc, ids, tables, small, first_ids, lane_block, W0_pairs, W0_mirror, W1, dense_t, W_top1, b_top1, W_top2, b_top2, W_top3,
          rotations, eye, same_row, out):
    n_small = small.shape[1] // SMALL_COLS
    n_picks = -(-n_small // PER_BANK)
    picks = [slice(g * PER_BANK, min((g + 1) * PER_BANK, n_small)) for g in range(n_picks)]
    ctx = ExitStack()
    with ctx:
        def sb(name, shape, dt=F32):
            return ctx.enter_context(nc.sbuf_tensor(name, shape, dt))

        def banks(name, n):
            return [ctx.enter_context(nc.psum_tensor(f"{name}{i}", [128, 512], F32)) for i in range(n)]

        def sem(name):
            return ctx.enter_context(nc.semaphore(name))

        ids_sb = sb("ids_sb", [TILE, TILES, FIELDS], I32)
        rot_f32 = sb("rot_f32", [ROWS, (1 + PASSES) * ROWS])
        rot = sb("rot", [ROWS, 1 + PASSES, ROWS], BF16)
        eye_sb = sb("eye_sb", [128, 128])
        eye_bf = sb("eye_bf", [128, 128], BF16)
        same_sb = sb("same_sb", [128, CHUNK])
        pair_w = sb("pair_w", [ROWS, PASSES, MAPS])
        mirror_w = sb("mirror_w", [ROWS, PASSES, MAPS])
        pair_hi = sb("pair_hi", [ROWS, PASSES, MAPS], F32R)
        pair_lo = sb("pair_lo", [ROWS, PASSES, MAPS], F32R)
        w1_sb = sb("w1_sb", [MAPS, FIELDS, MAPS])
        wt1 = sb("wt1", [128, 2, HID1])
        wt1_dense = sb("wt1_dense", [DENSE, HID1])
        wt2 = sb("wt2", [128, H1, HID2])
        wt3 = sb("wt3", [128, H2])
        bt1 = sb("bt1", [128, H1])
        bt2 = sb("bt2", [128, H2])
        dense_sb = sb("dense_sb", [DENSE, BATCH])


        emb = [sb(f"emb{i}", [TILE, FIELDS, DIM]) for i in range(2)]
        rest = sb("rest", [TILE, FIELDS, DIM])
        parts = sb("parts", [TILE, DIM, ROWS], BF16)
        parts_t = [sb(f"parts_t{i}", [ROWS, TILE, DIM], BF16) for i in range(2)]
        left = sb("left", [ROWS, TILE * DIM])
        prod = [sb(f"prod{i}", [ROWS, UNIT]) for i in range(BUFFERS)]
        prod_hi = [sb(f"prod_hi{i}", [ROWS, UNIT], F32R) for i in range(BUFFERS)]
        prod_lo = [sb(f"prod_lo{i}", [ROWS, UNIT], F32R) for i in range(BUFFERS)]
        x1 = sb("x1", [MAPS, TILE * DIM])
        turned = [sb(f"turned{i}", [128, MAPS + FIELDS]) for i in range(TURNED)]
        blocks = [sb(f"blocks{i}", [128, CHUNK, AUG]) for i in range(TURNED)]
        gram_flat = [sb(f"gram{i}", [MAPS, AUG * TILE]) for i in range(2)]
        gram = [g[:, :].rearrange("n (m b) -> n m b", b=TILE) for g in gram_flat]
        z2 = sb("z2", [MAPS, TILE])
        h1 = sb("h1", [128, H1, TILE])
        h2 = sb("h2", [128, H2, TILE])
        y_sb = sb("y_sb", [1, BATCH])

        lane_block_sb = sb("lane_block_sb", [128, 1 + SMALL_BLOCKS])
        block_id = sb("block_id", [TILE, n_small], I32)
        block_mask = sb("block_mask", [TILE, n_small, SMALL_BLOCKS])
        ids_cols, table_cols, pick_cols = n_small * TILE, n_small * SMALL_COLS, PER_BANK * SMALL_COLS
        one_hot = gram_flat[0][:, 0:ids_cols].rearrange("v (f b) -> v f b", b=TILE)
        lane_id = gram_flat[0][:, ids_cols:2 * ids_cols].bitcast(I32).rearrange("v (f b) -> v f b", b=TILE)
        small_sb = gram_flat[1][:, 0:table_cols].rearrange("v (f h d) -> v f h d", h=SMALL_BLOCKS, d=DIM)
        picked = [gram_flat[1][:, table_cols + i * pick_cols:table_cols + (i + 1) * pick_cols].rearrange(
            "b (f h d) -> b f h d", h=SMALL_BLOCKS, d=DIM) for i in range(2)]

        factors = Fills(banks("factors", 2))
        turns = Fills(banks("turns", 2))
        sums = Fills(banks("sums", 2))
        grams = Fills(banks("grams", 1))
        tops = Fills(banks("tops", 1))
        remainders, diagonals = {}, {}
        unit_bank = 0
        for s in STEPS:
            kind, t, i, k = s
            if kind == "rotate":
                factors.add(s, len(factors.number) % 2)
            if kind == "remainder":
                remainders[t, i, k] = len(remainders)
            if kind == "spread":
                diagonals[s] = len(diagonals)
            if kind in ("parts", "turn") or (kind == "rotate" and k == 0):
                turns.add(s, len(turns.number) % 2)
            if kind == "contract" and k == 0:
                unit_bank = 1 - unit_bank
            if kind == "contract" and k == PASSES - 1:
                sums.add(s, unit_bank)
            if kind == "hidden":
                over = t == TILES - 1
                sums.add(s, i % 2 if over else 1 - unit_bank)
            if kind == "gram":
                grams.add(s, 0)
            if (kind == "sum" and i == 0) or kind == "y":
                tops.add(s, 0)

        ids_in, consts_in, pairs_in = sem("ids_in"), sem("consts_in"), sem("pairs_in")
        w1_in, top_in, out_written = sem("w1_in"), sem("top_in"), sem("out_written")
        TOP_IN = 7 * 16
        first_ids_in = sem("first_ids_in")
        small_in = [sem(f"small_in{g}") for g in range(n_picks)]
        one_hot_ready = sem("one_hot_ready")
        picks_full = sem("picks_full")
        gathered = [sem(f"gathered{i}") for i in range(2)]
        small_picked = sem("small_picked")
        high_ready, rest_ready, mid_ready = sem("high_ready"), sem("rest_ready"), sem("mid_ready")
        own_step = sem("own_step")
        parts_ready = sem("parts_ready")
        consts_ready = sem("consts_ready")
        pair_w_ready = sem("pair_w_ready")
        factors_full, factors_out = sem("factors_full"), sem("factors_out")
        turns_full, turns_out = sem("turns_full"), sem("turns_out")
        sums_full, sums_out = sem("sums_full"), sem("sums_out")
        grams_full, grams_out = sem("grams_full"), sem("grams_out")
        tops_full, tops_out = sem("tops_full"), sem("tops_out")
        hi_ready = sem("hi_ready")
        lo_ready = sem("lo_ready")
        blocks_ready = sem("blocks_ready")

        block = ctx.enter_context(nc.Block())

        def unit(step):
            return slice(step[2] * UNIT, (step[2] + 1) * UNIT)

        def pass_rows(k):
            return slice(0, ROWS if k < PASSES - 1 else LAST_ROWS)

        def buffer(buffers, step):
            _, t, u, k = step
            return buffers[((t * UNITS + u) * PASSES + k) % BUFFERS]

        def part(i):
            return parts[:, :, i * FIELDS:(i + 1) * FIELDS].rearrange("b d m -> b m d")

        def chunk_buffer(buffers, step):
            return buffers[(step[1] * UNITS * UNIT_CHUNKS + step[2]) % TURNED]

        def pick_bank(g):
            return (factors.banks + turns.banks + sums.banks + grams.banks + tops.banks)[g]

        def batch_rows(t):
            return slice(t * TILE, (t + 1) * TILE)

        @block.sync
        def _(sp):
            sp.dma_start(ids_sb[:, :, :], ids.rearrange("(t p) f -> p t f", p=TILE)).then_inc(ids_in, 16)
            sp.dma_start(lane_block_sb[:, :], lane_block).then_inc(first_ids_in, 16)
            sp.dma_start(lane_id[:, :, :].rearrange("v f b -> v (f b)"),
                         first_ids.broadcast_to([128, n_small * TILE])).then_inc(first_ids_in, 16)
            sp.dma_start(rot_f32[:, :], rotations).then_inc(consts_in, 16)
            sp.dma_start(eye_sb[:, :], eye).then_inc(consts_in, 16)
            sp.dma_start(same_sb[:, :], same_row).then_inc(consts_in, 16)
            full = (PASSES - 1) * ROWS
            for dst, src in ((pair_w, W0_pairs), (mirror_w, W0_mirror)):
                sp.dma_start(dst[:, 0:PASSES - 1, :],
                             src[0:full, :].rearrange("(t p) o -> p t o", p=ROWS)).then_inc(pairs_in, 16)
                sp.dma_start(dst[0:LAST_ROWS, PASSES - 1, :], src[full:full + LAST_ROWS, :]).then_inc(pairs_in, 16)
            sp.dma_start(w1_sb[:, :, :], W1.rearrange("(m n) o -> n m o", n=MAPS)).then_inc(w1_in, 16)
            sp.dma_start(wt1[:, :, :], W_top1[0:2 * MAPS, :].rearrange("(k p) h -> p k h", p=128)).then_inc(top_in, 16)
            sp.dma_start(wt1_dense[:, :], W_top1[2 * MAPS:2 * MAPS + DENSE, :]).then_inc(top_in, 16)
            sp.dma_start(wt2[:, :, :], W_top2.rearrange("(k p) h -> p k h", p=128)).then_inc(top_in, 16)
            sp.dma_start(wt3[:, :], W_top3).then_inc(top_in, 16)
            sp.dma_start(bt1[:, :], b_top1).then_inc(top_in, 16)
            sp.dma_start(bt2[:, :], b_top2).then_inc(top_in, 16)
            sp.dma_start(dense_sb[:, :], dense_t).then_inc(top_in, 16)
            sp.wait_ge(tops_out, len(tops.number))
            sp.dma_start(out.rearrange("b one -> one b"), y_sb[:, :]).then_inc(out_written, 16)
            sp.wait_ge(out_written, 16)

        @block.gpsimd
        def _(pool):
            pool.wait_ge(ids_in, 16)
            for t in range(TILES):
                if t >= 2:
                    pool.wait_ge(rest_ready, t - 1)
                for f in range(n_small if t == 0 else 0, FIELDS):
                    nc.gpsimd.indirect_dma_start(
                        emb[t % 2][:, f, :], None, tables[f],
                        bass.IndirectOffsetOnAxis(ap=ids_sb[:, t, f:f + 1], axis=0)).then_inc(gathered[t % 2], 16)

        @block.vector
        def _(dve):
            own = 0

            def then_wait(ins):
                nonlocal own
                own += 1
                ins.then_inc(own_step, 1)
                dve.wait_ge(own_step, own)

            dve.wait_ge(first_ids_in, 32)
            for g, fs in enumerate(picks):
                then_wait(nc.vector.tensor_scalar(lane_id[:, fs, :], lane_id[:, fs, :], 127, None, ALU.bitwise_and))
                nc.vector.tensor_scalar(one_hot[:, fs, :], lane_id[:, fs, :], lane_block_sb[:, 0:1], None,
                                        ALU.is_equal).then_inc(one_hot_ready, 1)
            dve.wait_ge(ids_in, 16)
            then_wait(nc.vector.tensor_scalar(block_id[:, :], ids_sb[:, 0, 0:n_small], 7, None, ALU.logical_shift_right))
            then_wait(nc.vector.tensor_tensor(
                block_mask[:, :, :], block_id[:, :].unsqueeze(2).to_broadcast([TILE, n_small, SMALL_BLOCKS]),
                lane_block_sb[:, 1:].unsqueeze(1).to_broadcast([TILE, n_small, SMALL_BLOCKS]), ALU.is_equal))
            for g, fs in enumerate(picks):
                n = fs.stop - fs.start
                dve.wait_ge(picks_full, g + 1)
                then_wait(nc.vector.tensor_tensor(
                    picked[g % 2][:, 0:n, :, :],
                    pick_bank(g)[:, 0:n * SMALL_COLS].rearrange("b (f h d) -> b f h d", f=n, h=SMALL_BLOCKS),
                    block_mask[:, fs, :].unsqueeze(3).to_broadcast([TILE, n, SMALL_BLOCKS, DIM]), ALU.mult))
                then_wait(nc.vector.tensor_reduce(emb[0][:, fs, :], picked[g % 2][:, 0:n, :, :].rearrange("b f h d -> b f d h"),
                                                  mybir.AxisListType.X, ALU.add))
            dve.sem_inc(small_picked, 1)

            dve.wait_ge(consts_in, 48)
            nc.vector.tensor_copy(rot[:, :, :], rot_f32[:, :].rearrange("p (k q) -> p k q", q=ROWS)).then_inc(consts_ready, 1)
            nc.vector.tensor_copy(eye_bf[:, :], eye_sb[:, :]).then_inc(consts_ready, 1)
            for buf in blocks:
                nc.vector.tensor_copy(buf[:, :, FIELDS:AUG].rearrange("p c one -> p (c one)"), same_sb[:, :]).then_inc(consts_ready, 1)
            dve.wait_ge(pairs_in, 64)
            for rows, ks in ((slice(0, ROWS), slice(0, PASSES - 1)), (slice(0, LAST_ROWS), slice(PASSES - 1, PASSES))):
                then_wait(nc.vector.tensor_tensor(pair_w[rows, ks, :], pair_w[rows, ks, :], mirror_w[rows, ks, :], ALU.add))
                if ks.start == 0:
                    then_wait(nc.vector.tensor_scalar(pair_w[0:FIELDS, 0, :], pair_w[0:FIELDS, 0, :], 0.5, None, ALU.mult))
                then_wait(nc.vector.tensor_copy(pair_hi[rows, ks, :], pair_w[rows, ks, :]))
                then_wait(nc.vector.tensor_tensor(pair_lo[rows, ks, :], pair_w[rows, ks, :],
                                                  pair_hi[rows, ks, :].bitcast(F32), ALU.subtract))
            dve.sem_inc(pair_w_ready, 1)

            def split_embeddings(t, i):
                if i == 1:
                    dve.wait_ge(high_ready, t + 1)
                    nc.vector.tensor_tensor(rest[:, :, :], emb[t % 2][:, :, :], part(0), ALU.subtract).then_inc(rest_ready, 1)
                if i == 3:
                    dve.wait_ge(mid_ready, t + 1)
                    nc.vector.tensor_tensor(part(2), rest[:, :, :], part(1), ALU.subtract).then_inc(parts_ready, 1)

            def multiply_pairs(s):
                _, t, u, k = s
                rows = pass_rows(k)
                if k == 0:
                    dve.wait_ge(turns_out, turns.up_to(s))
                dve.wait_ge(factors_full, factors.up_to(s))
                nc.vector.tensor_tensor(buffer(prod, s)[rows, :], left[rows, unit(s)],
                                        factors.of[s][rows, :], ALU.mult).then_inc(factors_out, 1)

            def take_remainder(s):
                rows = pass_rows(s[3])
                dve.wait_ge(hi_ready, remainders[s[1:]] + 1)
                nc.vector.tensor_tensor(buffer(prod_lo, s)[rows, :], buffer(prod, s)[rows, :],
                                        buffer(prod_hi, s)[rows, :].bitcast(F32), ALU.subtract).then_inc(lo_ready, 1)

            def spread_fields(s):
                _, t, c, _ = s
                dve.wait_ge(turns_out, turns.up_to(("turn", t, c, 0)))
                fields = chunk_buffer(turned, s)[:, MAPS:MAPS + FIELDS]
                nc.vector.tensor_tensor(chunk_buffer(blocks, s)[:, :, 0:FIELDS],
                                        fields.unsqueeze(1).to_broadcast([128, CHUNK, FIELDS]),
                                        same_sb[:, :].unsqueeze(2).to_broadcast([128, CHUNK, FIELDS]),
                                        ALU.mult).then_inc(blocks_ready, 1)

            for s in STEPS:
                kind, t, i, k = s
                if kind == "split":
                    split_embeddings(t, i)
                if kind == "rotate":
                    multiply_pairs(s)
                if kind == "remainder":
                    take_remainder(s)
                if kind == "spread":
                    spread_fields(s)

        @block.scalar
        def _(act):
            for g, fs in enumerate(picks):
                act.dma_start(small_sb[:, fs, :, :].rearrange("v f h d -> v (f h d)"),
                              small[:, fs.start * SMALL_COLS:fs.stop * SMALL_COLS]).then_inc(small_in[g], 16)
            for s in STEPS:
                kind, t, i, k = s
                if kind == "split" and i == 0:
                    by_dma = (t // 2 + 1) * FIELDS - (n_small if t % 2 == 0 else 0)
                    act.wait_ge(gathered[t % 2], 16 * by_dma)
                    if t == 0:
                        act.wait_ge(small_picked, 1)
                    nc.scalar.copy(part(0), emb[t % 2][:, :, :]).then_inc(high_ready, 1)
                if kind == "split" and i == 2:
                    act.wait_ge(rest_ready, t + 1)
                    nc.scalar.copy(part(1), rest[:, :, :]).then_inc(mid_ready, 1)
                if kind == "parts":
                    act.wait_ge(turns_full, turns.up_to(s))
                    nc.scalar.copy(parts_t[t % 2][:, :, i * PART_D:(i + 1) * PART_D].rearrange("q b d -> q d b"),
                                   turns.of[s][0:ROWS, 0:PART_D * TILE // 2].bitcast(BF16).rearrange(
                                       "q (d b) -> q d b", b=TILE)).then_inc(turns_out, 1)
                if kind == "rotate" and k == 0:
                    act.wait_ge(turns_full, turns.up_to(s))
                    nc.scalar.copy(left[:, unit(s)], turns.of[s][0:ROWS, :]).then_inc(turns_out, 1)
                if kind == "round":
                    act.wait_ge(factors_out, factors.up_to(("rotate", t, i, k)))
                    nc.scalar.copy(buffer(prod_hi, s)[pass_rows(k), :], buffer(prod, s)[pass_rows(k), :]).then_inc(hi_ready, 1)
                if kind == "contract" and k == PASSES - 1:
                    act.wait_ge(sums_full, sums.up_to(s))
                    nc.scalar.copy(x1[:, unit(s)], sums.of[s][:, :]).then_inc(sums_out, 1)
                if kind == "turn":
                    act.wait_ge(turns_full, turns.up_to(s))
                    nc.scalar.copy(chunk_buffer(turned, s)[:, :], turns.of[s][:, 0:MAPS + FIELDS]).then_inc(turns_out, 1)
                if kind == "gram":
                    act.wait_ge(grams_full, grams.up_to(s))
                    nc.scalar.copy(gram[t % 2][:, :, i * CHUNK:(i + 1) * CHUNK],
                                   grams.of[s][:, 0:CHUNK * AUG].rearrange("n (b m) -> n m b", m=AUG)).then_inc(grams_out, 1)
                if kind == "sum" and i + SUM_GROUP >= FIELDS:
                    first = (kind, t, 0, 0)
                    act.wait_ge(tops_full, tops.up_to(first))
                    nc.scalar.copy(z2[:, :], tops.of[first][:, 0:TILE]).then_inc(tops_out, 1)
                if kind == "hidden":
                    h, bias, n = (h1, bt1, i) if i < H1 else (h2, bt2, i - H1)
                    act.wait_ge(top_in, TOP_IN)
                    act.wait_ge(sums_full, sums.up_to(s))
                    nc.scalar.activation(h[:, n, :], sums.of[s][:, 0:TILE], ACT.Relu, bias=bias[:, n:n + 1]).then_inc(sums_out, 1)
                if kind == "y":
                    act.wait_ge(tops_full, tops.up_to(s))
                    nc.scalar.copy(y_sb[:, batch_rows(t)], tops.of[s][0:1, 0:TILE]).then_inc(tops_out, 1)

        @block.tensor
        def _(pe):
            mm = nc.tensor.matmul

            def wait_free(fills, out_sem, s):
                if fills.before[s] is not None:
                    pe.wait_ge(out_sem, fills.before[s] + 1)

            def transpose_parts(s):
                _, t, g, _ = s
                pe.wait_ge(parts_ready, t + 1)
                wait_free(turns, turns_out, s)
                dst = turns.of[s][0:ROWS, 0:PART_D * TILE // 2].bitcast(BF16)
                for i in range(PART_D):
                    last = nc.tensor.transpose(dst[:, i * TILE:(i + 1) * TILE], parts[:, g * PART_D + i, :], eye_bf[:, :])
                last.then_inc(turns_full, 1)

            def rotate(s):
                _, t, u, k = s
                moving = parts_t[t % 2][:, u * UNIT_B:(u + 1) * UNIT_B, :].rearrange("q b d -> q (b d)")
                if k == 0:
                    pe.wait_ge(turns_out, turns.up_to(("parts", t, UNITS - 1, 0)))
                    wait_free(turns, turns_out, s)
                    mm(turns.of[s][0:ROWS, :], rot[:, 0, :], moving, start=True, stop=True).then_inc(turns_full, 1)
                wait_free(factors, factors_out, s)
                mm(factors.of[s][0:ROWS, :], rot[:, 1 + k, :], moving, start=True, stop=True).then_inc(factors_full, 1)

            def contract(s):
                _, t, u, k = s
                rows, source, fill = pass_rows(k), ("rotate", t, u, k), ("contract", t, u, PASSES - 1)
                if k == 0:
                    wait_free(sums, sums_out, fill)
                if k in SPLIT[t]:
                    pe.wait_ge(lo_ready, remainders[s[1:]] + 1)
                    hi, lo = buffer(prod_hi, source)[rows, :], buffer(prod_lo, source)[rows, :]
                    terms = [(pair_hi[rows, k, :], hi), (pair_lo[rows, k, :], hi), (pair_hi[rows, k, :], lo)]
                else:
                    pe.wait_ge(factors_out, factors.up_to(source))
                    terms = [(pair_w[rows, k, :], buffer(prod, source)[rows, :])]
                for n, (weights, moving) in enumerate(terms):
                    last = mm(sums.of[fill][:, :], weights, moving, start=(k == 0 and n == 0),
                              stop=(k == PASSES - 1 and n == len(terms) - 1))
                if k == PASSES - 1:
                    last.then_inc(sums_full, 1)

            def turn_over(s):
                _, t, c, _ = s
                cols = slice(c * CHUNK * DIM, (c + 1) * CHUNK * DIM)
                wait_free(turns, turns_out, s)
                chunk = parts_t[t % 2][:, c * CHUNK:(c + 1) * CHUNK, :].rearrange("q b d -> q (b d)")
                mm(turns.of[s][:, MAPS:MAPS + FIELDS], chunk, rot[:, 0, 0:FIELDS], start=True, stop=True)
                if c % UNIT_CHUNKS == 0:
                    pe.wait_ge(sums_out, sums.up_to(("contract", t, c // UNIT_CHUNKS, PASSES - 1)))
                nc.tensor.transpose(turns.of[s][:, 0:MAPS], x1[:, cols], eye_sb[:, :]).then_inc(turns_full, 1)

            def gram_block(s):
                _, t, c, _ = s
                wait_free(grams, grams_out, s)
                pe.wait_ge(blocks_ready, diagonals["spread", t, c, 0] + 1)
                mm(grams.of[s][:, 0:CHUNK * AUG], chunk_buffer(turned, s)[:, 0:MAPS],
                   chunk_buffer(blocks, s)[:, :, :].rearrange("p b m -> p (b m)"), start=True, stop=True).then_inc(grams_full, 1)

            def layer2(s):
                _, t, m0, _ = s
                acc = tops.of["sum", t, 0, 0][:, 0:TILE]
                if m0 == 0:
                    wait_free(tops, tops_out, s)
                    pe.wait_ge(w1_in, 16)
                    pe.wait_ge(grams_out, grams.up_to(("gram", t, UNITS * UNIT_CHUNKS - 1, 0)))
                for m in range(m0, min(m0 + SUM_GROUP, FIELDS)):
                    last = mm(acc, w1_sb[:, m, :], gram[t % 2][:, m, :], start=(m == 0), stop=(m == FIELDS - 1))
                if m == FIELDS - 1:
                    last.then_inc(tops_full, 1)

            def hidden(s):
                _, t, i, _ = s
                wait_free(sums, sums_out, s)
                acc = sums.of[s][:, 0:TILE]
                if i < H1:
                    cols = slice(i * 128, (i + 1) * 128)
                    pe.wait_ge(top_in, TOP_IN)
                    mm(acc, wt1[:, 0, cols], gram[t % 2][:, FIELDS, :], start=True, stop=False)
                    mm(acc, wt1_dense[:, cols], dense_sb[:, batch_rows(t)], start=False, stop=False)
                    pe.wait_ge(tops_out, tops.up_to(("sum", t, 0, 0)))
                    mm(acc, wt1[:, 1, cols], z2[:, :], start=False, stop=True).then_inc(sums_full, 1)
                else:
                    pe.wait_ge(sums_out, sums.up_to(("hidden", t, H1 - 1, 0)))
                    for j in range(H1):
                        last = mm(acc, wt2[:, j, (i - H1) * 128:(i - H1 + 1) * 128], h1[:, j, :], start=(j == 0), stop=(j == H1 - 1))
                    last.then_inc(sums_full, 1)

            def output(s):
                t = s[1]
                wait_free(tops, tops_out, s)
                pe.wait_ge(sums_out, sums.up_to(("hidden", t, H1 + H2 - 1, 0)))
                for j in range(H2):
                    last = mm(tops.of[s][0:1, 0:TILE], wt3[:, j:j + 1], h2[:, j, :], start=(j == 0), stop=(j == H2 - 1))
                last.then_inc(tops_full, 1)

            for g, fs in enumerate(picks):
                pe.wait_ge(small_in[g], 16)
                pe.wait_ge(one_hot_ready, g + 1)
                for n, f in enumerate(range(fs.start, fs.stop)):
                    last = mm(pick_bank(g)[:, n * SMALL_COLS:(n + 1) * SMALL_COLS], one_hot[:, f, :],
                              small_sb[:, f, :, :].rearrange("v h d -> v (h d)"), start=True, stop=True)
                last.then_inc(picks_full, 1)

            pe.wait_ge(consts_ready, 4)
            pe.wait_ge(pair_w_ready, 1)
            do = {"parts": transpose_parts, "rotate": rotate, "contract": contract, "turn": turn_over,
                  "gram": gram_block, "sum": layer2, "hidden": hidden, "y": output}
            for s in STEPS:
                if s[0] in do:
                    do[s[0]](s)


def kernel(**inputs):
    import numpy as np
    import concourse.bacc as bacc
    from concourse.bass_utils import run_bass_kernel_spmd

    field = np.arange(ROWS) % FIELDS
    distance = np.arange(ROWS) // FIELDS
    shifts = [0 * distance] + [PER_PASS * k + distance for k in range(PASSES)]
    rotations = np.concatenate([(field[:, None] == (field + s)[None, :] % FIELDS) for s in shifts], axis=1)
    eye = np.eye(128, dtype=np.float32)
    same_row = (np.arange(128)[:, None] // DIM == np.arange(CHUNK)[None, :])

    sizes = [inputs[f"tbl_{f}"].shape[0] for f in range(FIELDS)]
    order = [f for f in range(FIELDS) if sizes[f] <= 128 * SMALL_BLOCKS]
    n_small = len(order)
    order += [f for f in range(FIELDS) if sizes[f] > 128 * SMALL_BLOCKS]
    small = np.zeros((n_small, SMALL_BLOCKS * 128, DIM), np.float32)
    for i, f in enumerate(order[:n_small]):
        small[i, :sizes[f]] = np.asarray(inputs[f"tbl_{f}"])
    small = small.reshape(n_small, SMALL_BLOCKS, 128, DIM).transpose(2, 0, 1, 3).reshape(128, -1)
    ids = np.ascontiguousarray(np.asarray(inputs["ids"])[:, order])
    lane_block = np.concatenate([np.arange(128)[:, None], np.tile(np.arange(SMALL_BLOCKS), (128, 1))], axis=1)

    W0 = np.asarray(inputs["L0_rec_W0"]).reshape(FIELDS, FIELDS, MAPS)[order][:, order]
    m = np.tile(np.arange(FIELDS), SHIFTS)
    n = (m + np.repeat(np.arange(SHIFTS), FIELDS)) % FIELDS

    arrays = {
        "ids": ids,
        "small": np.ascontiguousarray(small),
        "first_ids": np.ascontiguousarray(ids[:TILE, :n_small].T).reshape(1, -1),
        "lane_block": lane_block.astype(np.float32),
        **{f"tbl_{f}": np.asarray(inputs[f"tbl_{f}"]) for f in range(FIELDS)},
        "W0_pairs": np.ascontiguousarray(W0[m, n]),
        "W0_mirror": np.ascontiguousarray(W0[n, m]),
        "W1": np.asarray(inputs["L0_rec_W1"]).reshape(FIELDS, MAPS, MAPS)[order].reshape(-1, MAPS),
        "dense_t": np.ascontiguousarray(np.asarray(inputs["dense_ctx"]).T),
        "W_top1": np.asarray(inputs["W_top1"]),
        "W_top2": np.asarray(inputs["W_top2"]),
        **{name: np.ascontiguousarray(np.asarray(inputs[name]).reshape(-1, 128).T)
           for name in ("b_top1", "b_top2", "W_top3")},
        "rotations": rotations.astype(np.float32),
        "eye": eye,
        "same_row": same_row.astype(np.float32),
    }
    nc = bacc.Bacc("TRN2", target_bir_lowering=False, num_devices=1)
    ap = {name: nc.dram_tensor(name, a.shape, mybir.dt.from_np(a.dtype), kind="ExternalInput").ap()
          for name, a in arrays.items()}
    out = nc.dram_tensor("out", (BATCH, 1), F32, kind="ExternalOutput").ap()
    build(nc, ap["ids"], [ap[f"tbl_{f}"] for f in order], ap["small"], ap["first_ids"], ap["lane_block"], ap["W0_pairs"], ap["W0_mirror"], ap["W1"],
          ap["dense_t"], ap["W_top1"], ap["b_top1"], ap["W_top2"], ap["b_top2"], ap["W_top3"],
          ap["rotations"], ap["eye"], ap["same_row"], out)
    result = run_bass_kernel_spmd(nc, [arrays], core_ids=[0])
    return result.results[0]["out"]
```

```python
from contextlib import ExitStack

import concourse.bass as bass
from concourse import mybir

F32 = mybir.dt.float32
F32R = mybir.dt.float32r
BF16 = mybir.dt.bfloat16
I32 = mybir.dt.int32
ALU = mybir.AluOpType
ACT = mybir.ActivationFunctionType

BATCH, FIELDS, DIM, MAPS = 512, 39, 16, 128
DENSE, HID1, HID2 = 16, 512, 256
H1, H2 = HID1 // 128, HID2 // 128
TILE = 128
TILES = BATCH // TILE
SHIFTS = FIELDS // 2 + 1
PER_PASS = 3
ROWS = PER_PASS * FIELDS
PASSES = -(-SHIFTS // PER_PASS)
LAST_ROWS = (SHIFTS - PER_PASS * (PASSES - 1)) * FIELDS
UNITS = 4
UNIT_B = TILE // UNITS
UNIT = UNIT_B * DIM
PART_D = 8
CHUNK = 128 // DIM
UNIT_CHUNKS = UNIT_B // CHUNK
AUG = FIELDS + 1
SMALL_BLOCKS = 10
SMALL_COLS = SMALL_BLOCKS * DIM
PER_BANK = 512 // SMALL_COLS
PICK_BANKS = 6
PICKS = 27
PICKED = 4

ALL = tuple(range(PASSES))
SPLIT = ((1, 3, 4, 6), ALL, ALL, ALL)
ROUND_LAG, REMAINDER_LAG, LAG = 1, 2, 4
BUFFERS = LAG + 1
PREPARE_AT = (22, 18, 16)
BEFORE_DMA = 3
HALF = 2
RIGHTS = 10
SUM_GROUP = 2
FINISH_AT = (13, 13, 13)
TURNED = 3


def by_dma(t):
    return t > 0


def rotated(t, u, k):
    return not by_dma(t) or (t == 1 and u == 0 and k < BEFORE_DMA)


def prepare_steps(t):
    first = [[("split", 0, i, 0)] for i in range(4)] if t == 0 else []
    return (first + [[("split", t, i, 1)] for i in range(4)] + [[]]
            + [[("parts", t, g, 0) for g in range(DIM // PART_D)]]
            + [[("left", t, u, 0) for u in range(HALF)]] * by_dma(t))


def chunk_steps(t, u):
    own = range(u * UNIT_CHUNKS, (u + 1) * UNIT_CHUNKS)
    stages = ("turn", "spread", "gram")
    return [[]] + [[(kind, t, c - n, 0) for n, kind in enumerate(stages) if c - n in own]
                   for c in range(own[0], own[-1] + len(stages))]


def finish_steps(t):
    return ([[("sum", t, m, 0)] for m in range(0, FIELDS, SUM_GROUP)]
            + [[("hidden", t, k, 0)] for k in range(H1 + H2)] + [[("y", t, 0, 0)]])


def schedule():
    steps = sum(prepare_steps(0), []) + [("fold", 0, 0, 0)]
    passes = [(t, u, k) for t in range(TILES) for u in range(UNITS) for k in range(PASSES)]
    prepare, chunks, finish = [], [], []
    at = 0
    while at < len(passes) + LAG or chunks or finish:
        t, i = divmod(at, UNITS * PASSES)
        if t + 1 < TILES and i == PREPARE_AT[t]:
            prepare = prepare_steps(t + 1)
        if 0 < t < TILES and i == FINISH_AT[t - 1]:
            finish = finish_steps(t - 1)
        if t < TILES and i == 0:
            steps += sum(prepare, [])
            prepare = []
        if at < len(passes):
            t, u, k = passes[at]
            if by_dma(t) and u % HALF == HALF - 1 and u + 1 < UNITS and k == 0:
                steps += [("left", t, u + 1 + n, 0) for n in range(HALF)]
            steps += [("left", t, u, 0)] * (k == 0 and not by_dma(t)) + [("rotate", t, u, k)] * rotated(t, u, k)
            steps.append(("multiply", t, u, k))
        for work in (prepare, finish, chunks):
            if work:
                steps += work.pop(0)
        for kind, lag in (("round", ROUND_LAG), ("remainder", REMAINDER_LAG)):
            if lag <= at < len(passes) + lag:
                t, u, k = passes[at - lag]
                if k in SPLIT[t]:
                    steps.append((kind, t, u, k))
        if LAG <= at < len(passes) + LAG:
            t, u, k = passes[at - LAG]
            steps.append(("contract", t, u, k))
            if k == PASSES - 1:
                chunks += chunk_steps(t, u)
        at += 1
    return steps + sum(finish_steps(TILES - 1), [])


STEPS = schedule()


def picked_tables(n_small):
    return [n_small, min(n_small, PICKS - n_small)] + [0] * (TILES - 2)


class Fills:

    def __init__(self, banks):
        self.banks, self.number, self.of, self.before, self.last = banks, {}, {}, {}, {}

    def add(self, step, bank):
        self.before[step] = self.last.get(bank)
        self.last[bank] = self.number[step] = len(self.number)
        self.of[step] = self.banks[bank]

    def up_to(self, step):
        return self.number[step] + 1


def build(nc, ids, tables, small, pick_ids, lane_block, W0_pairs, W0_mirror, W1, dense_t, W_top1, b_top1, W_top2, b_top2,
          W_top3, rotations, eye, same_row, out):
    n_small = small.shape[1] // SMALL_COLS
    n_picked = picked_tables(n_small)
    picks = [(t, f) for t in range(2) for f in range(n_picked[t])]
    groups = [slice(a, min(a + PER_BANK, len(picks))) for a in range(0, len(picks), PER_BANK)]

    def runs(n):
        return sum(len({t for t, _ in picks[g]}) for g in groups[:n])

    ctx = ExitStack()
    with ctx:
        def sb(name, shape, dt=F32):
            return ctx.enter_context(nc.sbuf_tensor(name, shape, dt))

        def banks(name, n):
            return [ctx.enter_context(nc.psum_tensor(f"{name}{i}", [128, 512], F32)) for i in range(n)]

        def sem(name):
            return ctx.enter_context(nc.semaphore(name))

        ids_sb = sb("ids_sb", [TILE, TILES, FIELDS], I32)
        rot = sb("rot", [ROWS, 1 + PASSES, ROWS], BF16)
        eye_sb = sb("eye_sb", [128, 128])
        eye_bf = sb("eye_bf", [128, 128], BF16)
        same_sb = sb("same_sb", [128, CHUNK])
        pair_w = sb("pair_w", [ROWS, PASSES, MAPS])
        pair_hi = sb("pair_hi", [ROWS, PASSES, MAPS], F32R)
        pair_lo = sb("pair_lo", [ROWS, PASSES, MAPS], F32R)
        w1_sb = sb("w1_sb", [MAPS, FIELDS, MAPS])
        wt1 = sb("wt1", [128, 2, HID1])
        wt1_dense = sb("wt1_dense", [DENSE, HID1])
        wt2 = sb("wt2", [128, H1, HID2])
        wt3 = sb("wt3", [128, H2])
        bt1 = sb("bt1", [128, H1])
        bt2 = sb("bt2", [128, H2])
        dense_sb = sb("dense_sb", [DENSE, BATCH])

        emb = [sb(f"emb{i}", [TILE, FIELDS, DIM]) for i in range(2)]
        rest = sb("rest", [TILE, FIELDS, DIM])
        parts = sb("parts", [TILE, DIM, ROWS], BF16)
        parts_t = [sb(f"parts_t{i}", [ROWS, TILE, DIM], BF16) for i in range(2)]
        left = sb("left", [ROWS, TILE * DIM])
        right = [sb(f"right{i}", [ROWS, HALF * UNIT]) for i in range(RIGHTS)]
        rot_f32 = right[0][:, 0:(1 + PASSES) * ROWS]
        mirror_w = right[1][:, 0:PASSES * MAPS].rearrange("p (k o) -> p k o", o=MAPS)
        prod = [sb(f"prod{i}", [ROWS, UNIT]) for i in range(BUFFERS)]
        prod_hi = [sb(f"prod_hi{i}", [ROWS, UNIT], F32R) for i in range(BUFFERS)]
        prod_lo = [sb(f"prod_lo{i}", [ROWS, UNIT], F32R) for i in range(BUFFERS)]
        x1 = sb("x1", [MAPS, TILE * DIM])
        turned = [sb(f"turned{i}", [128, MAPS + FIELDS]) for i in range(TURNED)]
        blocks = [sb(f"blocks{i}", [128, CHUNK, AUG]) for i in range(TURNED)]
        gram_flat = [sb(f"gram{i}", [MAPS, AUG * TILE]) for i in range(2)]
        gram = [g[:, :].rearrange("n (m b) -> n m b", b=TILE) for g in gram_flat]
        z2 = sb("z2", [MAPS, TILE])
        h1 = sb("h1", [128, H1, TILE])
        h2 = sb("h2", [128, H2, TILE])
        y_sb = sb("y_sb", [1, BATCH])

        lane_block_sb = sb("lane_block_sb", [128, 1 + SMALL_BLOCKS])
        block_id = sb("block_id", [TILE, len(picks)], I32)
        block_mask = sb("block_mask", [TILE, len(picks), SMALL_BLOCKS])
        pick_ids_sb = sb("pick_ids_sb", [len(picks), TILE], I32)
        lane_id = sb("lane_id", [len(picks), TILE], BF16)
        ids_cols, table_cols, pick_cols = len(picks) * TILE, n_small * SMALL_COLS, PER_BANK * SMALL_COLS
        one_hot = gram_flat[0][:, 0:ids_cols].rearrange("v (f b) -> v f b", b=TILE)
        small_sb = gram_flat[1][:, 0:table_cols].rearrange("v (f h d) -> v f h d", h=SMALL_BLOCKS, d=DIM)
        picked = [gram_flat[1][:, table_cols + i * pick_cols:table_cols + (i + 1) * pick_cols].rearrange(
            "b (f h d) -> b f h d", h=SMALL_BLOCKS, d=DIM) for i in range(PICKED)]

        factors = Fills(banks("factors", 2))
        turns = Fills(banks("turns", 2))
        sums = Fills(banks("sums", 2))
        grams = Fills(banks("grams", 1))
        tops = Fills(banks("tops", 1))
        splits, remainders, diagonals = {}, {}, {}
        unit_bank = 0
        for s in STEPS:
            kind, t, i, k = s
            if kind == "rotate":
                factors.add(s, len(factors.number) % 2)
            if kind == "split":
                splits[t, i, k] = len(splits) // 4 + 1
            if kind == "remainder":
                remainders[t, i, k] = len(remainders)
            if kind == "spread":
                diagonals[s] = len(diagonals)
            if kind in ("parts", "turn", "left"):
                turns.add(s, len(turns.number) % 2)
            if kind == "contract" and k == 0:
                unit_bank = 1 - unit_bank
            if kind == "contract" and k == PASSES - 1:
                sums.add(s, unit_bank)
            if kind == "hidden":
                over = t == TILES - 1
                sums.add(s, i % 2 if over else 1 - unit_bank)
            if kind == "gram":
                grams.add(s, 0)
            if (kind == "sum" and i == 0) or kind == "y":
                tops.add(s, 0)

        ids_in, consts_in, pairs_in = sem("ids_in"), sem("consts_in"), sem("pairs_in")
        w1_in, top_in, out_written = sem("w1_in"), sem("top_in"), sem("out_written")
        TOP_IN = 7 * 16
        pick_ids_in, eye_in = sem("pick_ids_in"), sem("eye_in")
        lane_ready = sem("lane_ready")
        lanes_full = sem("lanes_full")
        picks_out = sem("picks_out")
        small_in = [sem(f"small_in{g}") for g in range(-(-n_small // PER_BANK))]
        one_hot_ready = sem("one_hot_ready")
        picks_full = sem("picks_full")
        gathered = [sem(f"gathered{i}") for i in range(2)]
        small_picked = sem("small_picked")
        high_ready, rest_ready, mid_ready = sem("high_ready"), sem("rest_ready"), sem("mid_ready")
        own_step = sem("own_step")
        parts_ready = sem("parts_ready")
        consts_ready = sem("consts_ready")
        pair_w_ready = sem("pair_w_ready")
        factors_full = sem("factors_full")
        factors_in = [sem(f"factors_in{i}") for i in range(RIGHTS)]
        products_ready = sem("products_ready")
        contracted = sem("contracted")
        turns_full, turns_out = sem("turns_full"), sem("turns_out")
        sums_full, sums_out = sem("sums_full"), sem("sums_out")
        grams_full, grams_out = sem("grams_full"), sem("grams_out")
        tops_full, tops_out = sem("tops_full"), sem("tops_out")
        hi_ready = sem("hi_ready")
        lo_ready = sem("lo_ready")
        blocks_ready = sem("blocks_ready")

        block = ctx.enter_context(nc.Block())

        def unit(step):
            return slice(step[2] * UNIT, (step[2] + 1) * UNIT)

        def number(t, u, k):
            return (t * UNITS + u) * PASSES + k

        def distances(k):
            return range(k * PER_PASS, min((k + 1) * PER_PASS, SHIFTS))

        def right_number(t, u, k):
            return ((t - 1) * UNITS // HALF + u // HALF) * PASSES + k

        def right_dmas(n):
            return sum(len(distances(i % PASSES)) for i in range(n % RIGHTS, n + 1, RIGHTS))

        def pass_rows(k):
            return slice(0, ROWS if k < PASSES - 1 else LAST_ROWS)

        def buffer(buffers, step):
            _, t, u, k = step
            return buffers[((t * UNITS + u) * PASSES + k) % BUFFERS]

        def split_fields(step):
            _, t, _, large = step
            return slice(0, FIELDS) if t else slice(n_small, FIELDS) if large else slice(0, n_small)

        def part(i, fs):
            return parts[:, :, i * FIELDS + fs.start:i * FIELDS + fs.stop].rearrange("b d m -> b m d")

        def parts_copy(step):
            _, t, g, _ = step
            return (parts_t[t % 2][:, :, g * PART_D:(g + 1) * PART_D].rearrange("q b d -> q d b"),
                    turns.of[step][0:ROWS, 0:PART_D * TILE // 2].bitcast(BF16).rearrange("q (d b) -> q d b", b=TILE))

        def chunk_buffer(buffers, step):
            return buffers[(step[1] * UNITS * UNIT_CHUNKS + step[2]) % TURNED]

        def pick_bank(g):
            return (factors.banks + turns.banks + sums.banks)[g % PICK_BANKS]

        def lane_bank(g):
            return (grams.banks + tops.banks)[g % 2]

        def batch_rows(t):
            return slice(t * TILE, (t + 1) * TILE)

        @block.sync
        def _(sp):
            sp.dma_start(ids_sb[:, :, :], ids.rearrange("(t p) f -> p t f", p=TILE)).then_inc(ids_in, 16)
            sp.dma_start(pick_ids_sb[:, :], pick_ids).then_inc(pick_ids_in, 16)
            sp.dma_start(eye_sb[:, :], eye).then_inc(eye_in, 16)
            sp.dma_start(lane_block_sb[:, :], lane_block).then_inc(pick_ids_in, 16)
            for g in range(len(small_in)):
                fs = slice(g * PER_BANK, min((g + 1) * PER_BANK, n_small))
                sp.dma_start(small_sb[:, fs, :, :].rearrange("v f h d -> v (f h d)"),
                              small[:, fs.start * SMALL_COLS:fs.stop * SMALL_COLS]).then_inc(small_in[g], 16)
            sp.dma_start(rot_f32, rotations).then_inc(consts_in, 16)
            sp.dma_start(same_sb[:, :], same_row).then_inc(consts_in, 16)
            full = (PASSES - 1) * ROWS
            for dst, src in ((pair_w, W0_pairs), (mirror_w, W0_mirror)):
                sp.dma_start(dst[:, 0:PASSES - 1, :],
                             src[0:full, :].rearrange("(t p) o -> p t o", p=ROWS)).then_inc(pairs_in, 16)
                sp.dma_start(dst[0:LAST_ROWS, PASSES - 1, :], src[full:full + LAST_ROWS, :]).then_inc(pairs_in, 16)
            sp.dma_start(w1_sb[:, :, :], W1.rearrange("(m n) o -> n m o", n=MAPS)).then_inc(w1_in, 16)
            sp.dma_start(wt1[:, :, :], W_top1[0:2 * MAPS, :].rearrange("(k p) h -> p k h", p=128)).then_inc(top_in, 16)
            sp.dma_start(wt1_dense[:, :], W_top1[2 * MAPS:2 * MAPS + DENSE, :]).then_inc(top_in, 16)
            sp.dma_start(wt2[:, :, :], W_top2.rearrange("(k p) h -> p k h", p=128)).then_inc(top_in, 16)
            sp.dma_start(wt3[:, :], W_top3).then_inc(top_in, 16)
            sp.dma_start(bt1[:, :], b_top1).then_inc(top_in, 16)
            sp.dma_start(bt2[:, :], b_top2).then_inc(top_in, 16)
            sp.dma_start(dense_sb[:, :], dense_t).then_inc(top_in, 16)
            for s in STEPS:
                kind, t, u, _ = s
                if kind == "left" and by_dma(t) and u % HALF == HALF - 1:
                    sp.wait_ge(turns_out, turns.up_to(s))
                    cols = slice((u + 1 - HALF) * UNIT, (u + 1) * UNIT)
                    late = BEFORE_DMA if t == 1 and u < HALF else 0
                    for k in [*range(late, PASSES), *range(late)]:
                        n = right_number(t, u, k)
                        if n >= RIGHTS:
                            h, k0 = divmod(n - RIGHTS, PASSES)
                            sp.wait_ge(products_ready, number(1, h * HALF + HALF - 1, k0) + 1)
                        for j, d in enumerate(distances(k)):
                            sp.dma_start(right[n % RIGHTS][j * FIELDS:(j + 1) * FIELDS, :],
                                         left[d:d + FIELDS, cols]).then_inc(factors_in[n % RIGHTS], 16)
            sp.wait_ge(tops_out, len(tops.number))
            sp.dma_start(out.rearrange("b one -> one b"), y_sb[:, :]).then_inc(out_written, 16)
            sp.wait_ge(out_written, 16)

        @block.gpsimd
        def _(pool):
            pool.wait_ge(ids_in, 16)
            for t in range(TILES):
                if t >= 2:
                    pool.wait_ge(rest_ready, splits[t - 2, 1, 1])
                for f in range(n_picked[t], FIELDS):
                    nc.gpsimd.indirect_dma_start(
                        emb[t % 2][:, f, :], None, tables[f],
                        bass.IndirectOffsetOnAxis(ap=ids_sb[:, t, f:f + 1], axis=0)).then_inc(gathered[t % 2], 16)

        @block.vector
        def _(dve):
            own = 0

            def then_wait(ins):
                nonlocal own
                own += 1
                ins.then_inc(own_step, 1)
                dve.wait_ge(own_step, own)

            dve.wait_ge(pick_ids_in, 32)
            then_wait(nc.vector.tensor_scalar(pick_ids_sb[:, :], pick_ids_sb[:, :], 127, None, ALU.bitwise_and))
            nc.vector.tensor_copy(lane_id[:, :], pick_ids_sb[:, :]).then_inc(lane_ready, 1)
            dve.wait_ge(eye_in, 16)
            nc.vector.tensor_copy(eye_bf[:, :], eye_sb[:, :]).then_inc(lane_ready, 1)
            dve.wait_ge(ids_in, 16)
            for t in range(2):
                then_wait(nc.vector.tensor_scalar(block_id[:, t * n_small:t * n_small + n_picked[t]],
                                                  ids_sb[:, t, 0:n_picked[t]], 7, None, ALU.logical_shift_right))
            then_wait(nc.vector.tensor_tensor(
                block_mask[:, :, :], block_id[:, :].unsqueeze(2).to_broadcast([TILE, len(picks), SMALL_BLOCKS]),
                lane_block_sb[:, 1:].unsqueeze(1).to_broadcast([TILE, len(picks), SMALL_BLOCKS]), ALU.is_equal))

            def compare_lanes(i):
                g = groups[i]
                dve.wait_ge(lanes_full, i + 1)
                nc.vector.tensor_scalar(one_hot[:, g, :].rearrange("v f b -> v (f b)"),
                                        lane_bank(i)[:, 0:(g.stop - g.start) * TILE], lane_block_sb[:, 0:1], None,
                                        ALU.is_equal).then_inc(one_hot_ready, 1)

            def mask_blocks(i):
                g = groups[i]
                n = g.stop - g.start
                dve.wait_ge(picks_full, i + 1)
                if i >= PICKED:
                    dve.wait_ge(small_picked, runs(i - PICKED + 1))
                nc.vector.tensor_tensor(
                    picked[i % PICKED][:, 0:n, :, :],
                    pick_bank(i)[:, 0:n * SMALL_COLS].rearrange("b (f h d) -> b f h d", f=n, h=SMALL_BLOCKS),
                    block_mask[:, g, :].unsqueeze(3).to_broadcast([TILE, n, SMALL_BLOCKS, DIM]), ALU.mult).then_inc(picks_out, 1)

            def add_blocks(i):
                g = groups[i]
                dve.wait_ge(picks_out, i + 1)
                for t in range(2):
                    own_picks = [p for p in range(g.start, g.stop) if picks[p][0] == t]
                    if own_picks:
                        at, n, f = own_picks[0] - g.start, len(own_picks), picks[own_picks[0]][1]
                        nc.vector.tensor_reduce(
                            emb[t][:, f:f + n, :], picked[i % PICKED][:, at:at + n, :, :].rearrange("b f h d -> b f d h"),
                            mybir.AxisListType.X, ALU.add).then_inc(small_picked, 1)

            for i in range(len(groups) + 3):
                for stage, lag in ((compare_lanes, 0), (mask_blocks, 2), (add_blocks, 3)):
                    if 0 <= i - lag < len(groups):
                        stage(i - lag)

            dve.wait_ge(consts_in, 32)
            nc.vector.tensor_copy(rot[:, :, :], rot_f32.rearrange("p (k q) -> p k q", q=ROWS)).then_inc(consts_ready, 1)
            for buf in blocks:
                nc.vector.tensor_copy(buf[:, :, FIELDS:AUG].rearrange("p c one -> p (c one)"), same_sb[:, :]).then_inc(consts_ready, 1)
            def fold_weights():
                dve.wait_ge(pairs_in, 64)
                for rows, ks in ((slice(0, ROWS), slice(0, PASSES - 1)), (slice(0, LAST_ROWS), slice(PASSES - 1, PASSES))):
                    then_wait(nc.vector.tensor_tensor(pair_w[rows, ks, :], pair_w[rows, ks, :], mirror_w[rows, ks, :], ALU.add))
                    if ks.start == 0:
                        then_wait(nc.vector.tensor_scalar(pair_w[0:FIELDS, 0, :], pair_w[0:FIELDS, 0, :], 0.5, None, ALU.mult))
                    then_wait(nc.vector.tensor_copy(pair_hi[rows, ks, :], pair_w[rows, ks, :]))
                    then_wait(nc.vector.tensor_tensor(pair_lo[rows, ks, :], pair_w[rows, ks, :],
                                                      pair_hi[rows, ks, :].bitcast(F32), ALU.subtract))
                dve.sem_inc(pair_w_ready, 1)

            def split_embeddings(s):
                _, t, i, _ = s
                fs = split_fields(s)
                if i == 1:
                    dve.wait_ge(high_ready, splits[s[1:]])
                    nc.vector.tensor_tensor(rest[:, fs, :], emb[t % 2][:, fs, :], part(0, fs), ALU.subtract).then_inc(rest_ready, 1)
                if i == 3:
                    dve.wait_ge(mid_ready, splits[s[1:]])
                    nc.vector.tensor_tensor(part(2, fs), rest[:, fs, :], part(1, fs), ALU.subtract).then_inc(parts_ready, 1)

            def multiply_pairs(s):
                _, t, u, k = s
                rows = pass_rows(k)
                if k == 0:
                    dve.wait_ge(turns_out, turns.up_to(("left", t, u, 0)))
                if not rotated(t, u, k):
                    n = right_number(t, u, k)
                    dve.wait_ge(factors_in[n % RIGHTS], 16 * right_dmas(n))
                    factor = right[n % RIGHTS][rows, u % HALF * UNIT:(u % HALF + 1) * UNIT]
                    last = number(t, u, k) - BUFFERS
                    t0, u0, k0 = last // (UNITS * PASSES), last // PASSES % UNITS, last % PASSES
                    if k0 == PASSES - 1:
                        dve.wait_ge(sums_full, sums.up_to(("contract", t0, u0, k0)))
                    else:
                        dve.wait_ge(contracted, last - last // PASSES + 1)
                else:
                    factor = factors.of["rotate", t, u, k][rows, :]
                    dve.wait_ge(factors_full, factors.up_to(("rotate", t, u, k)))
                nc.vector.tensor_tensor(buffer(prod, s)[rows, :], left[rows, unit(s)], factor,
                                        ALU.mult).then_inc(products_ready, 1)

            def take_remainder(s):
                rows = pass_rows(s[3])
                dve.wait_ge(hi_ready, remainders[s[1:]] + 1)
                nc.vector.tensor_tensor(buffer(prod_lo, s)[rows, :], buffer(prod, s)[rows, :],
                                        buffer(prod_hi, s)[rows, :].bitcast(F32), ALU.subtract).then_inc(lo_ready, 1)

            def spread_fields(s):
                _, t, c, _ = s
                dve.wait_ge(turns_out, turns.up_to(("turn", t, c, 0)))
                fields = chunk_buffer(turned, s)[:, MAPS:MAPS + FIELDS]
                nc.vector.tensor_tensor(chunk_buffer(blocks, s)[:, :, 0:FIELDS],
                                        fields.unsqueeze(1).to_broadcast([128, CHUNK, FIELDS]),
                                        same_sb[:, :].unsqueeze(2).to_broadcast([128, CHUNK, FIELDS]),
                                        ALU.mult).then_inc(blocks_ready, 1)

            for s in STEPS:
                kind, t, i, k = s
                if kind == "split":
                    split_embeddings(s)
                if kind == "fold":
                    fold_weights()
                if kind == "multiply":
                    multiply_pairs(s)
                if kind == "remainder":
                    take_remainder(s)
                if kind == "spread":
                    spread_fields(s)

        @block.scalar
        def _(act):
            for s in STEPS:
                kind, t, i, k = s
                if kind == "split" and i == 0:
                    fs = split_fields(s)
                    if k:
                        fetched = sum(FIELDS - n_picked[u] for u in range(t % 2, t + 1, 2))
                        act.wait_ge(gathered[t % 2], 16 * fetched)
                    else:
                        act.wait_ge(small_picked, runs(len(groups)))
                    nc.scalar.copy(part(0, fs), emb[t % 2][:, fs, :]).then_inc(high_ready, 1)
                if kind == "split" and i == 2:
                    fs = split_fields(s)
                    act.wait_ge(rest_ready, splits[s[1:]])
                    nc.scalar.copy(part(1, fs), rest[:, fs, :]).then_inc(mid_ready, 1)
                if kind == "parts":
                    act.wait_ge(turns_full, turns.up_to(s))
                    nc.scalar.copy(*parts_copy(s)).then_inc(turns_out, 1)
                if kind == "left":
                    act.wait_ge(turns_full, turns.up_to(s))
                    if t:
                        act.wait_ge(products_ready, number(t - 1, i, PASSES - 1) + 1)
                    nc.scalar.copy(left[:, unit(s)], turns.of[s][0:ROWS, :]).then_inc(turns_out, 1)
                if kind == "round":
                    act.wait_ge(products_ready, number(t, i, k) + 1)
                    nc.scalar.copy(buffer(prod_hi, s)[pass_rows(k), :], buffer(prod, s)[pass_rows(k), :]).then_inc(hi_ready, 1)
                if kind == "contract" and k == PASSES - 1:
                    act.wait_ge(sums_full, sums.up_to(s))
                    nc.scalar.copy(x1[:, unit(s)], sums.of[s][:, :]).then_inc(sums_out, 1)
                if kind == "turn":
                    act.wait_ge(turns_full, turns.up_to(s))
                    nc.scalar.copy(chunk_buffer(turned, s)[:, :], turns.of[s][:, 0:MAPS + FIELDS]).then_inc(turns_out, 1)
                if kind == "gram":
                    act.wait_ge(grams_full, grams.up_to(s))
                    nc.scalar.copy(gram[t % 2][:, :, i * CHUNK:(i + 1) * CHUNK],
                                   grams.of[s][:, 0:CHUNK * AUG].rearrange("n (b m) -> n m b", m=AUG)).then_inc(grams_out, 1)
                if kind == "sum" and i + SUM_GROUP >= FIELDS:
                    first = (kind, t, 0, 0)
                    act.wait_ge(tops_full, tops.up_to(first))
                    nc.scalar.copy(z2[:, :], tops.of[first][:, 0:TILE]).then_inc(tops_out, 1)
                if kind == "hidden":
                    h, bias, n = (h1, bt1, i) if i < H1 else (h2, bt2, i - H1)
                    act.wait_ge(top_in, TOP_IN)
                    act.wait_ge(sums_full, sums.up_to(s))
                    nc.scalar.activation(h[:, n, :], sums.of[s][:, 0:TILE], ACT.Relu, bias=bias[:, n:n + 1]).then_inc(sums_out, 1)
                if kind == "y":
                    act.wait_ge(tops_full, tops.up_to(s))
                    nc.scalar.copy(y_sb[:, batch_rows(t)], tops.of[s][0:1, 0:TILE]).then_inc(tops_out, 1)

        @block.tensor
        def _(pe):
            mm = nc.tensor.matmul

            def wait_free(fills, out_sem, s):
                if fills.before[s] is not None:
                    pe.wait_ge(out_sem, fills.before[s] + 1)

            def transpose_parts(s):
                _, t, g, _ = s
                pe.wait_ge(parts_ready, splits[t, 3, 1])
                wait_free(turns, turns_out, s)
                dst = turns.of[s][0:ROWS, 0:PART_D * TILE // 2].bitcast(BF16)
                for i in range(PART_D):
                    last = nc.tensor.transpose(dst[:, i * TILE:(i + 1) * TILE], parts[:, g * PART_D + i, :], eye_bf[:, :])
                last.then_inc(turns_full, 1)

            def columns(t, u):
                return parts_t[t % 2][:, u * UNIT_B:(u + 1) * UNIT_B, :].rearrange("q b d -> q (b d)")

            def left_factor(s):
                _, t, u, _ = s
                pe.wait_ge(turns_out, turns.up_to(("parts", t, DIM // PART_D - 1, 0)))
                wait_free(turns, turns_out, s)
                mm(turns.of[s][0:ROWS, :], rot[:, 0, :], columns(t, u), start=True, stop=True).then_inc(turns_full, 1)

            def rotate(s):
                _, t, u, k = s
                wait_free(factors, products_ready, s)
                mm(factors.of[s][0:ROWS, :], rot[:, 1 + k, :], columns(t, u), start=True, stop=True).then_inc(factors_full, 1)

            def contract(s):
                _, t, u, k = s
                rows, fill = pass_rows(k), ("contract", t, u, PASSES - 1)
                if k == 0:
                    pe.wait_ge(pair_w_ready, 1)
                    wait_free(sums, sums_out, fill)
                if k in SPLIT[t]:
                    pe.wait_ge(lo_ready, remainders[s[1:]] + 1)
                    hi, lo = buffer(prod_hi, s)[rows, :], buffer(prod_lo, s)[rows, :]
                    terms = [(pair_hi[rows, k, :], hi), (pair_lo[rows, k, :], hi), (pair_hi[rows, k, :], lo)]
                else:
                    pe.wait_ge(products_ready, number(t, u, k) + 1)
                    terms = [(pair_w[rows, k, :], buffer(prod, s)[rows, :])]
                for n, (weights, moving) in enumerate(terms):
                    last = mm(sums.of[fill][:, :], weights, moving, start=(k == 0 and n == 0),
                              stop=(k == PASSES - 1 and n == len(terms) - 1))
                last.then_inc(sums_full if k == PASSES - 1 else contracted, 1)

            def turn_over(s):
                _, t, c, _ = s
                cols = slice(c * CHUNK * DIM, (c + 1) * CHUNK * DIM)
                wait_free(turns, turns_out, s)
                chunk = parts_t[t % 2][:, c * CHUNK:(c + 1) * CHUNK, :].rearrange("q b d -> q (b d)")
                mm(turns.of[s][:, MAPS:MAPS + FIELDS], chunk, rot[:, 0, 0:FIELDS], start=True, stop=True)
                if c % UNIT_CHUNKS == 0:
                    pe.wait_ge(sums_out, sums.up_to(("contract", t, c // UNIT_CHUNKS, PASSES - 1)))
                nc.tensor.transpose(turns.of[s][:, 0:MAPS], x1[:, cols], eye_sb[:, :]).then_inc(turns_full, 1)

            def gram_block(s):
                _, t, c, _ = s
                wait_free(grams, grams_out, s)
                pe.wait_ge(blocks_ready, diagonals["spread", t, c, 0] + 1)
                mm(grams.of[s][:, 0:CHUNK * AUG], chunk_buffer(turned, s)[:, 0:MAPS],
                   chunk_buffer(blocks, s)[:, :, :].rearrange("p b m -> p (b m)"), start=True, stop=True).then_inc(grams_full, 1)

            def layer2(s):
                _, t, m0, _ = s
                acc = tops.of["sum", t, 0, 0][:, 0:TILE]
                if m0 == 0:
                    wait_free(tops, tops_out, s)
                    pe.wait_ge(w1_in, 16)
                    pe.wait_ge(grams_out, grams.up_to(("gram", t, UNITS * UNIT_CHUNKS - 1, 0)))
                for m in range(m0, min(m0 + SUM_GROUP, FIELDS)):
                    last = mm(acc, w1_sb[:, m, :], gram[t % 2][:, m, :], start=(m == 0), stop=(m == FIELDS - 1))
                if m == FIELDS - 1:
                    last.then_inc(tops_full, 1)

            def hidden(s):
                _, t, i, _ = s
                wait_free(sums, sums_out, s)
                acc = sums.of[s][:, 0:TILE]
                if i < H1:
                    cols = slice(i * 128, (i + 1) * 128)
                    pe.wait_ge(top_in, TOP_IN)
                    mm(acc, wt1[:, 0, cols], gram[t % 2][:, FIELDS, :], start=True, stop=False)
                    mm(acc, wt1_dense[:, cols], dense_sb[:, batch_rows(t)], start=False, stop=False)
                    pe.wait_ge(tops_out, tops.up_to(("sum", t, 0, 0)))
                    mm(acc, wt1[:, 1, cols], z2[:, :], start=False, stop=True).then_inc(sums_full, 1)
                else:
                    pe.wait_ge(sums_out, sums.up_to(("hidden", t, H1 - 1, 0)))
                    for j in range(H1):
                        last = mm(acc, wt2[:, j, (i - H1) * 128:(i - H1 + 1) * 128], h1[:, j, :], start=(j == 0), stop=(j == H1 - 1))
                    last.then_inc(sums_full, 1)

            def output(s):
                t = s[1]
                wait_free(tops, tops_out, s)
                pe.wait_ge(sums_out, sums.up_to(("hidden", t, H1 + H2 - 1, 0)))
                for j in range(H2):
                    last = mm(tops.of[s][0:1, 0:TILE], wt3[:, j:j + 1], h2[:, j, :], start=(j == 0), stop=(j == H2 - 1))
                last.then_inc(tops_full, 1)

            pe.wait_ge(lane_ready, 2)
            for i in range(len(groups) + 1):
                if i < len(groups):
                    g = groups[i]
                    if i >= 2:
                        pe.wait_ge(one_hot_ready, i - 1)
                    for p in range(g.start, g.stop):
                        n = p - g.start
                        last = mm(lane_bank(i)[:, n * TILE:(n + 1) * TILE],
                                  eye_bf[0:len(picks), p:p + 1].to_broadcast([len(picks), 128]), lane_id[:, :],
                                  start=True, stop=True)
                    last.then_inc(lanes_full, 1)
                if i > 0:
                    i -= 1
                    g = groups[i]
                    if i < len(small_in):
                        pe.wait_ge(small_in[i], 16)
                    if i >= PICK_BANKS:
                        pe.wait_ge(picks_out, i - PICK_BANKS + 1)
                    pe.wait_ge(one_hot_ready, i + 1)
                    for p in range(g.start, g.stop):
                        n = p - g.start
                        last = mm(pick_bank(i)[:, n * SMALL_COLS:(n + 1) * SMALL_COLS], one_hot[:, p, :],
                                  small_sb[:, picks[p][1], :, :].rearrange("v h d -> v (h d)"), start=True, stop=True)
                    last.then_inc(picks_full, 1)
            pe.wait_ge(consts_ready, 1 + TURNED)
            do = {"parts": transpose_parts, "left": left_factor, "rotate": rotate, "contract": contract, "turn": turn_over,
                  "gram": gram_block, "sum": layer2, "hidden": hidden, "y": output}
            for s in STEPS:
                if s[0] in do:
                    do[s[0]](s)


def kernel(**inputs):
    import numpy as np
    import concourse.bacc as bacc
    from concourse.bass_utils import run_bass_kernel_spmd

    field = np.arange(ROWS) % FIELDS
    distance = np.arange(ROWS) // FIELDS
    shifts = [0 * distance] + [PER_PASS * k + distance for k in range(PASSES)]
    rotations = np.concatenate([(field[:, None] == (field + s)[None, :] % FIELDS) for s in shifts], axis=1)
    eye = np.eye(128, dtype=np.float32)
    same_row = (np.arange(128)[:, None] // DIM == np.arange(CHUNK)[None, :])

    sizes = [inputs[f"tbl_{f}"].shape[0] for f in range(FIELDS)]
    order = [f for f in range(FIELDS) if sizes[f] <= 128 * SMALL_BLOCKS]
    n_small = len(order)
    order += [f for f in range(FIELDS) if sizes[f] > 128 * SMALL_BLOCKS]
    small = np.zeros((n_small, SMALL_BLOCKS * 128, DIM), np.float32)
    for i, f in enumerate(order[:n_small]):
        small[i, :sizes[f]] = np.asarray(inputs[f"tbl_{f}"])
    small = small.reshape(n_small, SMALL_BLOCKS, 128, DIM).transpose(2, 0, 1, 3).reshape(128, -1)
    ids = np.ascontiguousarray(np.asarray(inputs["ids"])[:, order])
    pick_ids = np.concatenate([ids[t * TILE:(t + 1) * TILE, :n].T for t, n in enumerate(picked_tables(n_small))])
    lane_block = np.concatenate([np.arange(128)[:, None], np.tile(np.arange(SMALL_BLOCKS), (128, 1))], axis=1)

    W0 = np.asarray(inputs["L0_rec_W0"]).reshape(FIELDS, FIELDS, MAPS)[order][:, order]
    m = np.tile(np.arange(FIELDS), SHIFTS)
    n = (m + np.repeat(np.arange(SHIFTS), FIELDS)) % FIELDS

    arrays = {
        "ids": ids,
        "small": np.ascontiguousarray(small),
        "pick_ids": pick_ids,
        "lane_block": lane_block.astype(np.float32),
        **{f"tbl_{f}": np.asarray(inputs[f"tbl_{f}"]) for f in range(FIELDS)},
        "W0_pairs": np.ascontiguousarray(W0[m, n]),
        "W0_mirror": np.ascontiguousarray(W0[n, m]),
        "W1": np.asarray(inputs["L0_rec_W1"]).reshape(FIELDS, MAPS, MAPS)[order].reshape(-1, MAPS),
        "dense_t": np.ascontiguousarray(np.asarray(inputs["dense_ctx"]).T),
        "W_top1": np.asarray(inputs["W_top1"]),
        "W_top2": np.asarray(inputs["W_top2"]),
        **{name: np.ascontiguousarray(np.asarray(inputs[name]).reshape(-1, 128).T)
           for name in ("b_top1", "b_top2", "W_top3")},
        "rotations": rotations.astype(np.float32),
        "eye": eye,
        "same_row": same_row.astype(np.float32),
    }
    nc = bacc.Bacc("TRN2", target_bir_lowering=False, num_devices=1)
    ap = {name: nc.dram_tensor(name, a.shape, mybir.dt.from_np(a.dtype), kind="ExternalInput").ap()
          for name, a in arrays.items()}
    out = nc.dram_tensor("out", (BATCH, 1), F32, kind="ExternalOutput").ap()
    build(nc, ap["ids"], [ap[f"tbl_{f}"] for f in order], ap["small"], ap["pick_ids"], ap["lane_block"], ap["W0_pairs"], ap["W0_mirror"], ap["W1"],
          ap["dense_t"], ap["W_top1"], ap["b_top1"], ap["W_top2"], ap["b_top2"], ap["W_top3"],
          ap["rotations"], ap["eye"], ap["same_row"], out)
    result = run_bass_kernel_spmd(nc, [arrays], core_ids=[0])
    return result.results[0]["out"]
```
